# Optimizing a Trainium2 kernel written in Bass

```python
import numpy as np
import jax
import jax.numpy as jnp

def _softmax(x, axis=-1):
    return jax.nn.softmax(x, axis=axis)

def _gelu(x):
    return jax.nn.gelu(x, approximate=True)

def _silu(x):
    return jax.nn.silu(x)

def _sigmoid(x):
    return jax.nn.sigmoid(x)

def _layernorm(x, axis=-1, eps=1e-05):
    m = jnp.mean(x, axis=axis, keepdims=True)
    v = jnp.var(x, axis=axis, keepdims=True)
    return (x - m) / jnp.sqrt(v + eps)

def _scatter_add(tgt, idx, src, axis=0):
    return tgt.at[idx].add(src)

def _segment_sum(src, seg, n):
    return jax.ops.segment_sum(src, seg, n)
kernel_name = 'mk_adj_preln_d2_adj_r2_15b897'

def setup_inputs(seed: int=0):
    np.random.seed(seed)
    _w = jnp.asarray

    def _rec_inputs():
        import jax
        import jax.numpy as jnp
        _gk = jax.random.key(seed)
        x = -0.001547 + 1.001 * jax.random.normal(jax.random.fold_in(_gk, 1), (64, 128, 128), jnp.float32)
        _a = jax.random.bernoulli(jax.random.fold_in(_gk, 2), 0.125, (64, 128, 128))
        _a = jnp.logical_or(_a, jnp.swapaxes(_a, -1, -2))
        _a = jnp.logical_or(_a, jnp.eye(128, dtype=bool))
        adj = _a.astype(jnp.int32)
        return (x, adj)
    x, adj = _rec_inputs()

    def _L0_gnn_setup():
        import jax, jax.numpy as jnp
        import numpy as np
        EPS = 1e-05
        NEG = jnp.float32(-9000000000000000.0)

        def _leaky(z):
            return jnp.where(z >= 0, z, 0.01 * z)
        key = jax.random.key(seed)
        ks = jax.random.split(key, 12)
        B, N, d_in, d_hid, d_out = (4, 256, 128, 128, 128)
        d_mid = d_in // 2
        s = lambda fan: 1.0 / np.sqrt(fan)
        inp = {'x': jax.random.normal(ks[0], (B, N, d_in), dtype=jnp.float32), 'A_init': jax.random.randint(ks[1], (B, N, N), 0, 2, dtype=jnp.int32), 'W1': jax.random.normal(ks[2], (d_mid, d_in), dtype=jnp.float32) * s(d_in), 'b1': jnp.zeros((d_mid,), dtype=jnp.float32), 'g1': jnp.ones((d_mid,), dtype=jnp.float32), 'be1': jnp.zeros((d_mid,), dtype=jnp.float32), 'W2': jax.random.normal(ks[3], (1, d_mid), dtype=jnp.float32) * s(d_mid), 'b2': jnp.zeros((1,), dtype=jnp.float32), 'Wg': jax.random.normal(ks[4], (d_hid, d_in), dtype=jnp.float32) * s(d_in), 'bg': jnp.zeros((d_hid,), dtype=jnp.float32), 'gg': jnp.ones((d_hid,), dtype=jnp.float32), 'beg': jnp.zeros((d_hid,), dtype=jnp.float32), 'Wt': jax.random.normal(ks[5], (d_out, d_in + d_hid), dtype=jnp.float32) * s(d_in + d_hid), 'bt': jnp.zeros((d_out,), dtype=jnp.float32)}
        return inp
    _L0_gnn_all = _L0_gnn_setup()
    _L0_gnn_in = {k: v for k, v in _L0_gnn_all.items() if k in ('W1', 'b1', 'g1', 'be1', 'W2', 'b2', 'Wg', 'bg', 'gg', 'beg', 'Wt', 'bt')}
    del _L0_gnn_all

    def _L1_gnn_setup():
        import jax, jax.numpy as jnp
        import numpy as np
        B, N, F_IN, F_OUT = (8, 1024, 128, 128)
        ALPHA = 0.2
        NEG_INF = -9000000000000000.0
        key = jax.random.key(seed)
        k1, k2, k3, k4 = jax.random.split(key, 4)
        mag = 0.1
        inputs = jax.random.normal(k1, (B, N, F_IN), dtype=jnp.float32)
        adj = jax.random.randint(k2, (B, N, N), 0, 2, dtype=jnp.int32)
        W = jax.random.uniform(k3, (F_IN, F_OUT), dtype=jnp.float32, minval=-mag, maxval=mag)
        a = jax.random.uniform(k4, (2 * F_OUT, 1), dtype=jnp.float32, minval=-mag, maxval=mag)
        return {'inputs': inputs, 'adj': adj, 'W': W, 'a': a}
    _L1_gnn_all = _L1_gnn_setup()
    _L1_gnn_in = {k: v for k, v in _L1_gnn_all.items() if k in ('W', 'a')}
    del _L1_gnn_all
    return {'x': x, 'adj': adj, 'L0_gnn_W1': _L0_gnn_in['W1'], 'L0_gnn_b1': _L0_gnn_in['b1'], 'L0_gnn_g1': _L0_gnn_in['g1'], 'L0_gnn_be1': _L0_gnn_in['be1'], 'L0_gnn_W2': _L0_gnn_in['W2'], 'L0_gnn_b2': _L0_gnn_in['b2'], 'L0_gnn_Wg': _L0_gnn_in['Wg'], 'L0_gnn_bg': _L0_gnn_in['bg'], 'L0_gnn_gg': _L0_gnn_in['gg'], 'L0_gnn_beg': _L0_gnn_in['beg'], 'L0_gnn_Wt': _L0_gnn_in['Wt'], 'L0_gnn_bt': _L0_gnn_in['bt'], 'L1_gnn_W': _L1_gnn_in['W'], 'L1_gnn_a': _L1_gnn_in['a']}

def reference(x, adj, L0_gnn_W1, L0_gnn_b1, L0_gnn_g1, L0_gnn_be1, L0_gnn_W2, L0_gnn_b2, L0_gnn_Wg, L0_gnn_bg, L0_gnn_gg, L0_gnn_beg, L0_gnn_Wt, L0_gnn_bt, L1_gnn_W, L1_gnn_a):
    import jax
    import jax.numpy as jnp

    def _L0_gnn_ref(x, A_init, W1, b1, g1, be1, W2, b2, Wg, bg, gg, beg, Wt, bt):
        import jax, jax.numpy as jnp
        import numpy as np
        EPS = 1e-05
        NEG = jnp.float32(-9000000000000000.0)

        def _leaky(z):
            return jnp.where(z >= 0, z, 0.01 * z)
        D = jnp.abs(x[:, :, None, :] - x[:, None, :, :])
        h = jnp.einsum('bijc,oc->bijo', D, W1) + b1
        m = jnp.mean(h, axis=(0, 1, 2))
        v = jnp.mean((h - m) ** 2, axis=(0, 1, 2))
        h = (h - m) / jnp.sqrt(v + EPS) * g1 + be1
        h = _leaky(h)
        s = jnp.einsum('bijo,uo->biju', h, W2)[..., 0] + b2[0]
        s = jnp.where(A_init > 0, s, NEG)
        A = jax.nn.softmax(s, axis=-1)
        y = jnp.einsum('bij,bjc->bic', A, x)
        y = y @ Wg.T + bg
        mg = jnp.mean(y, axis=(0, 1))
        vg = jnp.mean((y - mg) ** 2, axis=(0, 1))
        y = (y - mg) / jnp.sqrt(vg + EPS) * gg + beg
        y = _leaky(y)
        out = jnp.concatenate([x, y], axis=2) @ Wt.T + bt
        return out

    def _L1_gnn_ref(inputs, adj, W, a):
        import jax, jax.numpy as jnp
        import numpy as np
        B, N, F_IN, F_OUT = (8, 1024, 128, 128)
        ALPHA = 0.2
        NEG_INF = -9000000000000000.0
        h = jnp.einsum('bnf,fo->bno', inputs, W)
        attn_self = h @ a[:F_OUT]
        attn_neigh = h @ a[F_OUT:]
        dense = attn_self + jnp.swapaxes(attn_neigh, 1, 2)
        dense = jnp.where(dense >= 0, dense, ALPHA * dense)
        attention = jnp.where(adj > 0, dense, NEG_INF)
        attention = jax.nn.softmax(attention, axis=1)
        h_prime = jnp.einsum('bnm,bmo->bno', attention, h)
        return jax.nn.elu(h_prime)
    h = jnp.maximum(_layernorm(x, axis=-1), 0.0)
    x = x + _L0_gnn_ref(h, adj, L0_gnn_W1, L0_gnn_b1, L0_gnn_g1, L0_gnn_be1, L0_gnn_W2, L0_gnn_b2, L0_gnn_Wg, L0_gnn_bg, L0_gnn_gg, L0_gnn_beg, L0_gnn_Wt, L0_gnn_bt)
    h = jnp.maximum(_layernorm(x, axis=-1), 0.0)
    x = x + _L1_gnn_ref(h, adj, L1_gnn_W, L1_gnn_a)
    return x

_drawn_inputs = setup_inputs


def setup_inputs(seed=0):
    import zlib

    import numpy as np

    out = dict(_drawn_inputs(seed))
    spreads = {'L0_gnn_b1': (0.0, 0.8),
     'L0_gnn_g1': (1.0, 0.2),
     'L0_gnn_be1': (0.0, 0.405),
     'L0_gnn_bg': (0.0, 0.8),
     'L0_gnn_gg': (1.0, 0.2),
     'L0_gnn_beg': (0.0, 0.1),
     'L0_gnn_bt': (0.0, 0.1)}
    factors = {}
    for name, (base, spread) in spreads.items():
        noise = np.random.default_rng([zlib.crc32(name.encode()), seed]).standard_normal(out[name].shape)
        drawn = base * np.exp(spread * noise) if base else spread * noise
        out[name] = jnp.asarray(drawn.astype(out[name].dtype))
    for name, factor in factors.items():
        out[name] = (out[name] * factor).astype(out[name].dtype)
    return out
```

```python
from contextlib import ExitStack

import numpy as np

import concourse.bass as bass
from concourse import mybir

F32 = mybir.dt.float32
I32 = mybir.dt.int32
ALU = mybir.AluOpType
ACT = mybir.ActivationFunctionType
AX = mybir.AxisListType

B, N, C = 64, 128, 128
MID = 64
EPS = 1e-5
NEG = -9e15
SLOPE0, SLOPE1 = 0.01, 0.2
QUAD = 4
NQ = B // QUAD
PAIRS = float(B * N * N)

BLK = 8
NBLK = N // BLK
WIDE = 1024
BANK = 512
DIAG = 7
LAST = 8
CHUNKS = [[k, NBLK - 2 - k] for k in range(DIAG)] + [None, [DIAG]]
NCH = len(CHUNKS)
TILES = [2] * LAST + [1]
FLAT = sum(TILES) * BANK
PER = 2 * NCH
ROUNDS = 5
ROUND_END = [1, 3, 5, 7, 8]
SLOTS = 6
LAG = 2


def strip(block):
    return BLK * (block + 1), N - BLK * (block + 1)


def two_layers(nc, x, adj, adj_t, w1, w1_tt, wg_t, wt1_t, wt2_t, l1_w, l1_wt, cols, bt_rows,
               ident_in, fold_in, half_in, out):
    flat = nc.dram_tensor("score_rows", [B, FLAT], F32, kind="Internal").ap()
    x_n = x.rearrange("b n c -> n b c")
    out_n = out.rearrange("b n c -> n b c")
    adj_n = adj.rearrange("b i j -> i b j")
    adj_tn = adj_t.rearrange("b j i -> j b i")

    with ExitStack() as ctx:
        def sb(name, shape, dt=F32):
            return ctx.enter_context(nc.sbuf_tensor(name, shape, dt))

        def sem(name):
            return ctx.enter_context(nc.semaphore(name))

        w1_sb = sb("w1_sb", [MID, C])
        w1tt_sb = sb("w1tt_sb", [C, 2 * MID])
        wg_sb = sb("wg_sb", [C, C])
        wt1_sb = sb("wt1_sb", [C, C])
        wt2_sb = sb("wt2_sb", [C, C])
        l1w_sb = sb("l1w_sb", [C, C])
        l1wt_sb = sb("l1wt_sb", [C, C])
        col = sb("col", [128, 10])
        G1, BE1, B1, W2, BG, GG, BEG, A1, A2, B2 = (col[:, n:n + 1] for n in range(10))
        bt_sb = sb("bt_sb", [128, C])
        ident = sb("ident", [128, 128])
        fold = sb("fold", [128, 128])
        half = sb("half", [128, NBLK, BLK])
        minus_half = sb("minus_half", [128, 16])
        ones = sb("ones", [MID, 128])
        h_nat = sb("h_nat", [N, B, C])
        h_tr = sb("h_tr", [C, B, N])
        diff = [sb(f"diff{s}", [C, 2, WIDE]) for s in range(SLOTS)]
        relu = [sb(f"relu{s}", [128, WIDE]) for s in range(SLOTS)]
        sum_d = sb("sum_d", [128, NQ * PER])
        sum_q = sb("sum_q", [128, NQ * PER])
        st = sb("st", [128, 32])
        w2_rows = sb("w2_rows", [128, 32])
        lin_rows = sb("lin_rows", [C, 2, 32])
        w1a = sb("w1a", [C, 128])
        w2a_c = sb("w2a_c", [C, 1])
        s_row = [sb(f"s_row{p}", [128, ROUNDS, BANK]) for p in range(2)]
        s_up = sb("s_up", [N, QUAD, N])
        s_dg = sb("s_dg", [N, QUAD, BLK])
        s_all = sb("s_all", [N, QUAD, N])
        s_all2 = sb("s_shift", [N, QUAD, N])
        adj_sb = sb("adj_sb", [N, QUAD, N], I32)
        mneg = sb("mneg", [N, QUAD, N])
        prob = sb("prob", [N, QUAD, N])
        prob_tr = sb("prob_tr", [N, QUAD, N])
        h_q = sb("h_q", [N, QUAD, C])
        mix = sb("mix", [C, QUAD, N])
        rows = sb("rows", [N, 3, QUAD])
        bst = sb("bst", [C, NQ, 6])
        bag = sb("bag", [C, 8])

        psum = ctx.enter_context(nc.psum_tensor("psum", [128, 8, BANK], F32))
        prod = [psum[:, 2 * n:2 * n + 2, :] for n in range(3)]
        score = [psum[:, 6, :], psum[:, 7, :]]
        att = [psum[:, 4, :].rearrange("p (b n) -> p b n", b=QUAD),
               psum[:, 5, :].rearrange("p (b n) -> p b n", b=QUAD)]

        weights_in = sem("weights_in")
        x_in = [sem(f"x_in{g}") for g in range(4)]
        dve_ln = sem("dve_ln")
        centred = sem("centred")
        squared = sem("squared")
        var_ready = sem("var_ready")
        rstd_ready = sem("rstd_ready")
        h_ready = sem("h_ready")
        turned = sem("turned")
        h_tr_ready = sem("h_tr_ready")
        consts_set = sem("consts_set")
        wa_mm = sem("wa_mm")
        wa_ready = sem("wa_ready")

        diff_ready = [sem("diff_ready1"), sem("diff_ready2")]
        abs_ready = [sem("abs_ready1"), sem("abs_ready2")]
        prod_ready = [sem("prod_ready1"), sem("prod_ready2")]
        squares_done = sem("squares_done")
        relu_ready = sem("relu_ready")
        shift_mm = sem("shift_mm")
        shift_ready = sem("shift_ready")
        stat = sem("stat")
        stat_sums = sem("stat_sums")
        stat_mm = sem("stat_mm")
        stat_var = sem("stat_var")
        stat_rstd = sem("stat_rstd")
        stat_lin = sem("stat_lin")
        stat_lin_mm = sem("stat_lin_mm")
        pass2_ready = sem("pass2_ready")
        round_done = sem("round_done")
        row_ready = sem("row_ready")
        rows_stored = [sem("rows_stored0"), sem("rows_stored1")]
        s_up_clear = sem("s_up_clear")
        s_in = sem("s_in")
        adj_in = sem("adj_in")
        hq_in = sem("hq_in")
        diag_set = sem("diag_set")
        s_half_ready = sem("s_half_ready")
        mask_ready = sem("mask_ready")
        s_sum = sem("s_sum")
        s_masked = sem("s_masked")
        dve_att = sem("dve_att")
        s_shifted = sem("s_shifted")
        exp_done = sem("exp_done")
        prob_ready = sem("prob_ready")
        prob_turned = sem("prob_turned")
        prob_tr_ready = sem("prob_tr_ready")
        mixed = sem("mixed")
        mix_ready = sem("mix_ready")
        y_mm = sem("y_mm")
        y_ready = sem("y_ready")
        bn2 = sem("bn2")
        bn2_var = sem("bn2_var")
        bn2_rstd = sem("bn2_rstd")
        bn2_ready = sem("bn2_ready")

        final = final_tiles(nc, sb, sem, dict(diff=diff, psum=psum))

        block = ctx.enter_context(nc.Block())

        def sc(n):
            return st[:, n:n + 1]

        def chunk_at(i, k):
            return i * PER + k

        def ln_sum(g):
            return sum_d[:, 16 * g:16 * g + 16]

        def ln_sq(g):
            return sum_d[:, 64 + 16 * g:80 + 16 * g]

        def ln_var(g):
            return sum_d[:, 128 + 16 * g:144 + 16 * g]

        def ln_rstd(g):
            return sum_d[:, 192 + 16 * g:208 + 16 * g]

        def group(g):
            return h_nat[:, 16 * g:16 * g + 16, :]

        def sq_tile(g):
            return diff[g][:, :, :].rearrange("p a (b c) -> p (a b) c", c=C)

        def bcast(v, n):
            return v.unsqueeze(2).broadcast_to([v.shape[0], v.shape[1], n])

        def tr_tile(g):
            return psum[:, 4 * (g % 2):4 * (g % 2) + 4, :]

        def rounds_before(i, k):
            back = 0
            if k < 0:
                k += PER
                back = 1
            c, m = divmod(k, NCH)
            r = next(n for n, e in enumerate(ROUND_END) if m <= e)
            return (i - back) * 2 * ROUNDS + c * ROUNDS + r + 1

        @block.sync
        def _(sp):
            for g in range(4):
                sp.dma_start(h_nat[:, 16 * g:16 * g + 16, :], x_n[:, 16 * g:16 * g + 16, :]).then_inc(x_in[g], 16)

            def store_rows(i, c):
                sp.wait_ge(row_ready, (i * 2 + c + 1) * ROUNDS)
                for g in range(2):
                    dst = flat[bass.ds(i * QUAD + 2 * c + g, 1), :]
                    for q in range(4):
                        sp.dma_start(dst[:, 0:16 * BANK].rearrange("b (r q x) -> b r q x", q=4, x=BANK)[:, :, q, :],
                                     s_row[c][32 * q + g:32 * q + g + 1, 0:4, :]).then_inc(rows_stored[c], 16)
                    sp.dma_start(dst[:, 16 * BANK:FLAT],
                                 s_row[c][g:g + 1, 4, :]).then_inc(rows_stored[c], 16)

            def load_scores(i, first):
                if not first:
                    sp.wait_ge(s_half_ready, i)
                else:
                    sp.wait_ge(s_up_clear, 1)
                for c in range(2):
                    sp.wait_ge(rows_stored[c], (i + 1) * 10 * 16)
                src = flat[bass.ds(i * QUAD, QUAD), :]
                for k, blocks in enumerate(CHUNKS):
                    at = k * WIDE
                    if blocks is None:
                        sp.dma_start(s_dg[:, :, :], src[:, at:at + WIDE].rearrange("b (p j) -> p b j", j=BLK))\
                          .then_inc(s_in, 16)
                        continue
                    for blk in blocks:
                        j0, n = strip(blk)
                        sp.dma_start(s_up[BLK * blk:BLK * blk + BLK, :, j0:N],
                                     src[:, at:at + BLK * n].rearrange("b (p j) -> p b j", j=n))\
                          .then_inc(s_in, 16)
                        at += BLK * n

            def load_graphs(i, first):
                if not first:
                    sp.wait_ge(mask_ready, i)
                    sp.wait_ge(mixed, i)
                sp.dma_start(adj_sb[:, :, :], adj_n[:, bass.ds(i * QUAD, QUAD), :]).then_inc(adj_in, 16)
                sp.dma_start(h_q[:, :, :], h_nat[:, bass.ds(i * QUAD, QUAD), :]).then_inc(hq_in, 16)

            def graphs(i, first):
                store_rows(i, 0)
                load_graphs(i, first)
                store_rows(i, 1)
                load_scores(i, first)

            graphs(0, True)
            with sp.Fori(1, NQ) as i:
                graphs(i, False)
            final["sync"](sp, x_n, out_n, adj_tn, h_tr, y_ready)

        @block.gpsimd
        def _(pool):
            nc.gpsimd.memset(minus_half[:, :], -0.5)
            nc.gpsimd.memset(ones[:, :], 1.0)
            nc.gpsimd.memset(w2_rows[:, :], 0.0)
            nc.gpsimd.memset(lin_rows[:, :, :], 0.0).then_inc(consts_set, 1)
            nc.gpsimd.memset(s_up[:, :, :], 0.0).then_inc(s_up_clear, 1)
            pool.wait_ge(consts_set, 1)
            for g in range(4):
                pool.wait_ge(var_ready, g + 1)
                nc.gpsimd.tensor_tensor(ln_rstd(g), ln_var(g), minus_half[:, 0:16], ALU.pow).then_inc(rstd_ready, 1)
            pool.wait_ge(stat_var, 1)
            nc.gpsimd.tensor_tensor(sc(11), sc(10), minus_half[:, 0:1], ALU.pow).then_inc(stat_rstd, 1)

            def assemble(i):
                pool.wait_ge(weights_in, 16 * 12)
                pool.wait_ge(s_in, (i + 1) * 16 * 16)
                if not isinstance(i, int) or i > 0:
                    pool.wait_ge(s_sum, i)
                nc.gpsimd.tensor_tensor(s_all[:, :, :].rearrange("p b (k j) -> p b k j", j=BLK),
                                        s_dg[:, :, :].unsqueeze(2).broadcast_to([N, QUAD, NBLK, BLK]),
                                        half[:, :, :].unsqueeze(1).broadcast_to([N, QUAD, NBLK, BLK]),
                                        ALU.mult).then_inc(diag_set, 1)
                pool.wait_ge(adj_in, (i + 1) * 16)
                if not isinstance(i, int) or i > 0:
                    pool.wait_ge(s_masked, i)
                pool.wait_ge(diag_set, i + 1)
                nc.gpsimd.tensor_tensor(s_all[:, :, :], s_all[:, :, :], s_up[:, :, :], ALU.add)\
                  .then_inc(s_half_ready, 1)
                nc.gpsimd.tensor_scalar(mneg[:, :, :], adj_sb[:, :, :], 0.0, NEG, ALU.is_le, ALU.mult)\
                  .then_inc(mask_ready, 1)

            assemble(0)
            with pool.Fori(1, NQ) as i:
                assemble(i)
            pool.wait_ge(bn2_var, 1)
            nc.gpsimd.tensor_tensor(bag[:, 3:4], bag[:, 2:3], minus_half[:, 0:1], ALU.pow).then_inc(bn2_rstd, 1)
            final["gpsimd"](pool, bt_sb, minus_half)

        @block.scalar
        def _(act):
            for t, src in ((w1_sb, w1), (w1tt_sb, w1_tt), (wg_sb, wg_t), (wt1_sb, wt1_t), (wt2_sb, wt2_t),
                           (l1w_sb, l1_w), (l1wt_sb, l1_wt), (col, cols), (bt_sb, bt_rows),
                           (ident, ident_in), (fold, fold_in)):
                act.dma_start(t[:, :], src).then_inc(weights_in, 16)
            act.dma_start(half[:, :, :], half_in).then_inc(weights_in, 16)
            for g in range(4):
                act.wait_ge(centred, g + 1)
                nc.scalar.activation(sq_tile(g), group(g), ACT.Square).then_inc(squared, 1)
                if g > 0:
                    act.wait_ge(turned, g)
                    nc.scalar.copy(h_tr[:, 16 * g - 16:16 * g, :], tr_tile(g - 1)).then_inc(h_tr_ready, 1)
            act.wait_ge(turned, 4)
            nc.scalar.copy(h_tr[:, 48:64, :], tr_tile(3)).then_inc(h_tr_ready, 1)

            def absolute(phase, i, k):
                n = WIDE if k % NCH != LAST else BANK
                act.wait_ge(diff_ready[phase], chunk_at(i, k) + 1)
                tile = diff[k % SLOTS][:, :, 0:n]
                acc = sum_d[:, bass.ds(chunk_at(i, k), 1)] if phase == 0 else None
                nc.scalar.activation(tile, tile, ACT.Abs, accum_out=acc).then_inc(abs_ready[phase], 1)

            def square(i, k):
                t = TILES[k % NCH]
                act.wait_ge(prod_ready[0], chunk_at(i, k) + 1)
                tile = prod[k % 3][:, 0:t, :]
                nc.scalar.activation(tile, tile, ACT.Square, bias=sc(0),
                                     accum_out=sum_q[:, bass.ds(chunk_at(i, k), 1)]).then_inc(squares_done, 1)

            def pass1_body(i, first):
                for k in range(PER):
                    absolute(0, i, k)
                    if first and k == 1:
                        act.wait_ge(shift_ready, 1)
                    if k > 0:
                        square(i, k - 1)
                    elif not first:
                        square(i - 1, PER - 1)

            pass1_body(0, True)
            with act.Fori(1, NQ) as i:
                pass1_body(i, False)
            square(NQ - 1, PER - 1)

            def rectify(i, k):
                t = TILES[k % NCH]
                act.wait_ge(prod_ready[1], chunk_at(i, k) + 1)
                if not (isinstance(i, int) and i == 0 and k < SLOTS):
                    act.wait_ge(round_done, rounds_before(i, k - SLOTS))
                nc.scalar.activation(relu[k % SLOTS][:, 0:t * BANK], prod[k % 2][:, 0:t, :].rearrange("p a b -> p (a b)"),
                                     ACT.Relu, bias=sc(14), scale=sc(12)).then_inc(relu_ready, 1)

            def exps(i):
                act.wait_ge(s_shifted, i + 1)
                nc.scalar.activation(prob[:, :, :], s_all2[:, :, :], ACT.Exp).then_inc(exp_done, 1)

            def pass2_body(i, first):
                for k in range(PER):
                    absolute(1, i, k)
                    if k > 0:
                        rectify(i, k - 1)
                    elif not first:
                        rectify(i - 1, PER - 1)
                    if k == 10 and not first:
                        exps(i - 1)

            act.wait_ge(pass2_ready, 1)
            pass2_body(0, True)
            with act.Fori(1, NQ) as i:
                pass2_body(i, False)
            rectify(NQ - 1, PER - 1)
            exps(NQ - 1)
            final["scalar"](act, bag)

        @block.tensor
        def _(pe):
            pe.wait_ge(weights_in, 16 * 12)
            nc.tensor.matmul(psum[:, 0, 0:1], l1wt_sb[:, :], A1, start=True, stop=True)
            nc.tensor.matmul(psum[:, 0, 1:2], l1wt_sb[:, :], A2, start=True, stop=True).then_inc(wa_mm, 1)
            pe.wait_ge(wa_ready, 1)
            for g in range(4):
                pe.wait_ge(h_ready, g + 1)
                if g >= 2:
                    pe.wait_ge(h_tr_ready, g - 1)
                for b in range(16):
                    last = nc.tensor.transpose(tr_tile(g)[:, b // 4, 128 * (b % 4):128 * (b % 4) + 128],
                                               h_nat[:, 16 * g + b, :], ident[:, :])
                last.then_inc(turned, 1)
            pe.wait_ge(h_tr_ready, 4)

            def products(phase, i, k, nbuf):
                pe.wait_ge(abs_ready[phase], chunk_at(i, k) + 1)
                for t in range(TILES[k % NCH]):
                    for g in range(2):
                        last = nc.tensor.matmul(prod[k % nbuf][MID * g:MID * g + MID, t, :], w1tt_sb[:, 0:MID],
                                                diff[k % SLOTS][:, g, t * BANK:t * BANK + BANK],
                                                start=True, stop=True)
                last.then_inc(prod_ready[phase], 1)

            def pass1_body(i, first):
                for k in range(PER):
                    if not (first and k < 3):
                        pe.wait_ge(squares_done, chunk_at(i, k) - 2)
                    products(0, i, k, 3)
                    if first and k == 0:
                        nc.tensor.matmul(score[0][:, 0:1], w1tt_sb[:, :], sum_d[:, 0:1],
                                         start=True, stop=True).then_inc(shift_mm, 1)

            pass1_body(0, True)
            with pe.Fori(1, NQ) as i:
                pass1_body(i, False)

            pe.wait_ge(stat_sums, 1)
            nc.tensor.matmul(score[0][:, 1:2], w1tt_sb[:, :], sc(3), start=True, stop=True)
            nc.tensor.matmul(score[0][:, 2:3], fold[:, :], sc(6), start=True, stop=True).then_inc(stat_mm, 1)
            pe.wait_ge(stat_lin, 1)
            nc.tensor.matmul(score[0][:, 3:4], w1_sb[:, :], st[0:MID, 16:17], start=True, stop=True)
            nc.tensor.matmul(score[0][:, 4:5], ones[:, :], st[0:MID, 17:18], start=True, stop=True).then_inc(stat_lin_mm, 1)
            pe.wait_ge(pass2_ready, 1)

            def scores(i, c, r, first):
                done = c * ROUNDS + r
                if not (first and done < 2):
                    pe.wait_ge(row_ready, i * 2 * ROUNDS + done - 1)
                pe.wait_ge(relu_ready, chunk_at(i, c * NCH + ROUND_END[r]) + 1)
                tiles = range(4) if r < ROUNDS - 1 else range(1)
                bank = score[done % 2]
                for part in range(3):
                    for q in tiles:
                        k = c * NCH + (4 * r + q) // 2
                        t = q % 2
                        if part == 0:
                            w, m = w2_rows[:, :], relu[k % SLOTS][:, t * BANK:t * BANK + BANK]
                        else:
                            w, m = lin_rows[:, part - 1, :], diff[k % SLOTS][:, part - 1, t * BANK:t * BANK + BANK]
                        last = nc.tensor.matmul(bank[32 * q:32 * q + 32, :], w, m, start=(part == 0), stop=(part == 2),
                                                tile_position=(0, 32 * q))
                last.then_inc(round_done, 1)

            def att_sum(i):
                pe.wait_ge(s_half_ready, i + 1)
                for b in range(QUAD):
                    nc.tensor.matmul(att[0][:, b, :], ident[:, :], s_all[:, b, :], start=True, stop=False)
                    last = nc.tensor.matmul(att[0][:, b, :], s_all[:, b, :], ident[:, :], start=False, stop=True)
                last.then_inc(s_sum, 1)

            def att_turn(i):
                pe.wait_ge(prob_ready, i + 1)
                for b in range(QUAD):
                    last = nc.tensor.transpose(att[1][:, b, :], prob[:, b, :], ident[:, :])
                last.then_inc(prob_turned, 1)

            def att_mix(i):
                pe.wait_ge(prob_tr_ready, i + 1)
                pe.wait_ge(hq_in, (i + 1) * 16)
                for b in range(QUAD):
                    last = nc.tensor.matmul(att[0][:, b, :], h_q[:, b, :], prob_tr[:, b, :], start=True, stop=True)
                last.then_inc(mixed, 1)

            def att_out(i):
                pe.wait_ge(mix_ready, i + 1)
                nc.tensor.matmul(psum[:, 5, :], wg_sb[:, :], mix[:, :, :].rearrange("p b n -> p (b n)"),
                                 start=True, stop=True).then_inc(y_mm, 1)

            ATT = {8: att_sum, 12: att_turn, 14: att_mix, 16: att_out}

            def pass2_body(i, first):
                for k in range(PER):
                    if not (first and k < 2):
                        pe.wait_ge(relu_ready, chunk_at(i, k) - 1)
                    products(1, i, k, 2)
                    m = k - LAG
                    if m >= 0 and m % NCH in ROUND_END:
                        scores(i, m // NCH, ROUND_END.index(m % NCH), first)
                    elif m < 0 and not first and (m + PER) % NCH in ROUND_END:
                        scores(i - 1, 1, ROUND_END.index((m + PER) % NCH), False)
                    if k in ATT and not first:
                        ATT[k](i - 1)

            pass2_body(0, True)
            with pe.Fori(1, NQ) as i:
                pass2_body(i, False)
            for m in range(PER - LAG, PER):
                scores(NQ - 1, 1, ROUND_END.index(m % NCH), False)
            for k in sorted(ATT):
                ATT[k](NQ - 1)
            final["tensor"](pe, dict(wt1=wt1_sb, wt2=wt2_sb, l1w=l1w_sb, w1a=w1a, w2a=w2a_c, ident=ident))

        @block.vector
        def _(dve):
            count = [0]

            def ln_step(ins):
                count[0] += 1
                ins.then_inc(dve_ln, 1)
                return count[0]

            def centre(g):
                dve.wait_ge(x_in[g], 16)
                dve.wait_ge(dve_ln, ln_step(nc.vector.tensor_reduce(ln_sum(g), group(g), AX.X, ALU.add)))
                dve.wait_ge(dve_ln, ln_step(nc.vector.tensor_scalar(ln_sum(g), ln_sum(g), 1.0 / C, None, ALU.mult)))
                nc.vector.tensor_tensor(group(g), group(g), bcast(ln_sum(g), C), ALU.subtract).then_inc(centred, 1)

            def scale(g):
                dve.wait_ge(squared, g + 1)
                dve.wait_ge(dve_ln, ln_step(nc.vector.tensor_reduce(ln_sq(g), sq_tile(g), AX.X, ALU.add)))
                nc.vector.tensor_scalar(ln_var(g), ln_sq(g), 1.0 / C, EPS, ALU.mult, ALU.add).then_inc(var_ready, 1)
                dve.wait_ge(rstd_ready, g + 1)
                nc.vector.scalar_tensor_tensor(group(g), group(g), 0.0, bcast(ln_rstd(g), C), ALU.max, ALU.mult)\
                  .then_inc(h_ready, 1)

            dve.wait_ge(wa_mm, 1)
            dve.wait_ge(weights_in, 16 * 12)
            nc.vector.tensor_copy(w1a[:, :], psum[:, 0, 0:1].broadcast_to([C, 128]))
            nc.vector.tensor_copy(w2a_c[:, :], psum[:, 0, 1:2]).then_inc(wa_ready, 1)
            centre(0)
            for g in range(4):
                if g < 3:
                    centre(g + 1)
                scale(g)
            dve.wait_ge(h_tr_ready, 4)

            def differences(phase, i, k):
                if not (isinstance(i, int) and i == 0 and k < SLOTS):
                    if phase == 0:
                        dve.wait_ge(prod_ready[0], chunk_at(i, k) - SLOTS + 1)
                    else:
                        dve.wait_ge(round_done, rounds_before(i, k - SLOTS))
                c, m = divmod(k, NCH)
                tile = diff[k % SLOTS]
                two = h_tr[:, bass.ds(i * QUAD + 2 * c, 2), :]
                if CHUNKS[m] is None:
                    for g in range(2):
                        one = h_tr[:, bass.ds(i * QUAD + 2 * c + g, 1), :].rearrange("p a (k j) -> p (a k) j", j=BLK)
                        last = nc.vector.tensor_tensor(
                            tile[:, g, :].rearrange("p (k i j) -> p k i j", i=BLK, j=BLK),
                            one.unsqueeze(2).broadcast_to([C, NBLK, BLK, BLK]),
                            one.unsqueeze(3).broadcast_to([C, NBLK, BLK, BLK]), ALU.subtract)
                    last.then_inc(diff_ready[phase], 1)
                    return
                at = 0
                for blk in CHUNKS[m]:
                    j0, n = strip(blk)
                    last = nc.vector.tensor_tensor(
                        tile[:, :, at:at + BLK * n].rearrange("p a (i j) -> p a i j", j=n),
                        two[:, :, j0:N].unsqueeze(2).broadcast_to([C, 2, BLK, n]),
                        two[:, :, j0 - BLK:j0].unsqueeze(3).broadcast_to([C, 2, BLK, n]), ALU.subtract)
                    at += BLK * n
                last.then_inc(diff_ready[phase], 1)

            def pass1_body(i, first):
                for k in range(PER):
                    differences(0, i, k)
                    if first and k == 2:
                        dve.wait_ge(shift_mm, 1)
                        nc.vector.tensor_scalar(sc(0), score[0][:, 0:1], -0.5 / WIDE, None, ALU.mult)\
                          .then_inc(shift_ready, 1)

            pass1_body(0, True)
            with dve.Fori(1, NQ) as i:
                pass1_body(i, False)

            done = [0]

            def then(ins):
                done[0] += 1
                ins.then_inc(stat, 1)
                dve.wait_ge(stat, done[0])

            dve.wait_ge(squares_done, NQ * PER)
            v_d = sum_d[:, :].rearrange("p (q k) -> p q k", k=NCH)[:, :, DIAG]
            v_q = sum_q[:, :].rearrange("p (q k) -> p q k", k=NCH)[:, :, DIAG]
            nc.vector.tensor_reduce(sc(1), sum_d[:, :], AX.X, ALU.add)
            nc.vector.tensor_reduce(sc(2), v_d, AX.X, ALU.add)
            nc.vector.tensor_reduce(sc(4), sum_q[:, :], AX.X, ALU.add)
            then(nc.vector.tensor_reduce(sc(5), v_q, AX.X, ALU.add))
            nc.vector.scalar_tensor_tensor(sc(3), sc(1), 2.0, sc(2), ALU.mult, ALU.subtract)
            nc.vector.scalar_tensor_tensor(sc(6), sc(4), 2.0, sc(5), ALU.mult, ALU.subtract).then_inc(stat_sums, 1)
            dve.wait_ge(stat_mm, 1)
            then(nc.vector.tensor_scalar(sc(7), score[0][:, 1:2], 1.0 / PAIRS, None, ALU.mult))
            then(nc.vector.tensor_tensor(sc(8), sc(7), sc(0), ALU.add))
            then(nc.vector.tensor_tensor(sc(9), sc(8), sc(8), ALU.mult))
            then(nc.vector.scalar_tensor_tensor(sc(9), score[0][:, 2:3], 1.0 / PAIRS, sc(9), ALU.mult, ALU.subtract))
            nc.vector.tensor_scalar(sc(10), sc(9), EPS, None, ALU.add).then_inc(stat_var, 1)
            dve.wait_ge(stat_rstd, 1)
            then(nc.vector.tensor_tensor(sc(12), sc(11), G1, ALU.mult))
            then(nc.vector.tensor_tensor(sc(13), sc(7), B1, ALU.add))
            then(nc.vector.tensor_tensor(sc(13), B1, sc(13), ALU.subtract))
            then(nc.vector.tensor_tensor(sc(14), sc(13), sc(12), ALU.mult))
            then(nc.vector.tensor_tensor(sc(14), sc(14), BE1, ALU.add))
            then(nc.vector.tensor_scalar(sc(15), W2, SLOPE0, None, ALU.mult))
            nc.vector.tensor_tensor(sc(16), sc(15), sc(12), ALU.mult)
            nc.vector.tensor_tensor(sc(17), sc(15), sc(14), ALU.mult).then_inc(stat_lin, 1)
            for g in range(2):
                part = slice(MID * g, MID * g + MID)
                nc.vector.tensor_scalar(w2_rows[part, g:g + 1], col[part, 3:4], 1.0 - SLOPE0, None, ALU.mult)
            dve.wait_ge(stat_lin_mm, 1)
            for g in range(2):
                nc.vector.tensor_copy(lin_rows[:, g, g:g + 1], score[0][:, 3:4])
            nc.vector.tensor_tensor(sc(18), score[0][:, 4:5], B2, ALU.add).then_inc(pass2_ready, 1)
            dve.wait_ge(pass2_ready, 1)

            def evacuate(i, c, r):
                dve.wait_ge(round_done, i * 2 * ROUNDS + c * ROUNDS + r + 1)
                if not (isinstance(i, int) and i == 0):
                    dve.wait_ge(rows_stored[c], i * 160)
                p = 128 if r < ROUNDS - 1 else 32
                nc.vector.tensor_copy(s_row[c][0:p, r, :], score[(c * ROUNDS + r) % 2][0:p, :]).then_inc(row_ready, 1)

            def link(i, n, ins):
                ins.then_inc(dve_att, 1)
                dve.wait_ge(dve_att, i * 4 + n)

            def att_scores(i):
                dve.wait_ge(s_sum, i + 1)
                dve.wait_ge(mask_ready, i + 1)
                nc.vector.scalar_tensor_tensor(s_all2[:, :, :], att[0], sc(18), mneg[:, :, :], ALU.add, ALU.add)\
                  .then_inc(s_masked, 1)
                dve.wait_ge(s_masked, i + 1)
                link(i, 1, nc.vector.tensor_reduce(rows[:, 0, :], s_all2[:, :, :], AX.X, ALU.max))
                nc.vector.tensor_tensor(s_all2[:, :, :], s_all2[:, :, :], bcast(rows[:, 0, :], N), ALU.subtract)\
                  .then_inc(s_shifted, 1)

            def att_norm(i):
                dve.wait_ge(exp_done, i + 1)
                link(i, 2, nc.vector.tensor_reduce(rows[:, 1, :], prob[:, :, :], AX.X, ALU.add))
                link(i, 3, nc.vector.reciprocal(rows[:, 2, :], rows[:, 1, :]))
                nc.vector.tensor_tensor(prob[:, :, :], prob[:, :, :], bcast(rows[:, 2, :], N), ALU.mult)\
                  .then_inc(prob_ready, 1)

            def att_copy(i):
                dve.wait_ge(prob_turned, i + 1)
                nc.vector.tensor_copy(prob_tr[:, :, :], att[1]).then_inc(prob_tr_ready, 1)

            def att_mix(i):
                dve.wait_ge(mixed, i + 1)
                nc.vector.tensor_copy(mix[:, :, :], att[0]).then_inc(mix_ready, 1)

            def att_y(i):
                dve.wait_ge(y_mm, i + 1)
                y = h_nat[:, bass.ds(i * QUAD, QUAD), :]
                link(i, 4, nc.vector.tensor_scalar(y, att[1], BG, None, ALU.add))
                nc.vector.bn_stats(bst[:, bass.ds(i, 1), :].rearrange("p a s -> p (a s)"),
                                   y.rearrange("p b n -> p (b n)")).then_inc(y_ready, 1)

            ATT = {9: att_scores, 11: att_norm, 13: att_copy, 15: att_mix, 17: att_y}

            def pass2_body(i, first):
                for k in range(PER):
                    differences(1, i, k)
                    m = k - LAG - 1
                    if m >= 0 and m % NCH in ROUND_END:
                        evacuate(i, m // NCH, ROUND_END.index(m % NCH))
                    elif m < 0 and not first and (m + PER) % NCH in ROUND_END:
                        evacuate(i - 1, 1, ROUND_END.index((m + PER) % NCH))
                    if k in ATT and not first:
                        ATT[k](i - 1)

            pass2_body(0, True)
            with dve.Fori(1, NQ) as i:
                pass2_body(i, False)
            for m in range(PER - LAG - 1, PER):
                if m % NCH in ROUND_END:
                    evacuate(NQ - 1, 1, ROUND_END.index(m % NCH))
            for k in sorted(ATT):
                ATT[k](NQ - 1)

            def then2(n, ins):
                ins.then_inc(bn2, 1)
                dve.wait_ge(bn2, n)

            dve.wait_ge(y_ready, NQ)
            then2(1, nc.vector.bn_aggr(bag[:, 0:2], bst[:, :, :].rearrange("p q s -> p (q s)")))
            nc.vector.tensor_scalar(bag[:, 2:3], bag[:, 1:2], EPS, None, ALU.add).then_inc(bn2_var, 1)
            dve.wait_ge(bn2_rstd, 1)
            then2(2, nc.vector.tensor_tensor(bag[:, 4:5], bag[:, 3:4], GG, ALU.mult))
            then2(3, nc.vector.tensor_tensor(bag[:, 5:6], bag[:, 0:1], bag[:, 4:5], ALU.mult))
            nc.vector.tensor_tensor(bag[:, 6:7], BEG, bag[:, 5:6], ALU.subtract).then_inc(bn2_ready, 1)
            final["vector"](dve, h_nat, bag, bn2_ready)


def final_tiles(nc, sb, sem, old):
    NI = B // 8
    diff, psum = old["diff"], old["psum"]

    def tiles(s):
        return [diff[s][:, n // 2, 512 * (n % 2):512 * (n % 2) + 512].rearrange("p (b n) -> p b n", b=4)
                for n in range(4)]

    T = [tiles(3 * q) + tiles(3 * q + 1) + tiles(3 * q + 2) for q in range(2)]
    X, H, Y, X1, SQ, H2, H2T, DEN, MN, HWN, MIN, OUT = range(12)
    adjt = [sb(f"adjt{q}", [128, 4, 128], I32) for q in range(2)]
    small = [sb(f"small{q}", [128, 10, 4]) for q in range(2)]

    def bank(q, n):
        return psum[:, 4 * q + n, :].rearrange("p (b n) -> p b n", b=4)

    names = ["x_q", "h_q2", "adjt_q", "y_act", "y_leaky", "o_mm", "x_bt", "x1", "ln_c", "ln_sq", "ln_var", "ln_rstd", "h2",
             "h2_turned", "h2t", "lin_mm", "mask", "den", "shifted", "expd", "hwn", "att_mm", "min", "minexp", "out_ready",
             "stored", "link"]
    s = {n: [sem(f"f_{n}{q}") for q in range(2)] for n in names}

    def bc(v, n=128):
        return v.unsqueeze(2).broadcast_to([v.shape[0], v.shape[1], n])

    def sync(sp, x_n, out_n, adj_tn, h_tr, y_ready):
        sp.wait_ge(y_ready, NQ)

        def loads(i, first):
            for q in range(2):
                g = bass.ds(i * 8 + 4 * q, 4)
                if not first:
                    sp.wait_ge(s["x1"][q], i)
                sp.dma_start(T[q][X], x_n[:, g, :]).then_inc(s["x_q"][q], 16)
                if not first:
                    sp.wait_ge(s["o_mm"][q], i)
                sp.dma_start(T[q][H], h_tr[:, g, :]).then_inc(s["h_q2"][q], 16)
                if not first:
                    sp.wait_ge(s["mask"][q], i)
                sp.dma_start(adjt[q][:, :, :], adj_tn[:, g, :]).then_inc(s["adjt_q"][q], 16)

        def stores(i):
            for q in range(2):
                sp.wait_ge(s["out_ready"][q], i + 1)
                sp.dma_start(out_n[:, bass.ds(i * 8 + 4 * q, 4), :], T[q][OUT]).then_inc(s["stored"][q], 16)

        loads(0, True)
        with sp.Fori(1, NI) as i:
            loads(i, False)
            stores(i - 1)
        stores(NI - 1)
        for q in range(2):
            sp.wait_ge(s["stored"][q], 16 * NI)

    def gpsimd(pool, bt_sb, minus_half):
        def body(i, first):
            for q in range(2):
                pool.wait_ge(s["adjt_q"][q], (i + 1) * 16)
                if not first:
                    pool.wait_ge(s["shifted"][q], i)
                pool.wait_ge(s["x_q"][q], (i + 1) * 16)
                nc.gpsimd.tensor_tensor(T[q][X], T[q][X], bt_sb[:, :].unsqueeze(1).broadcast_to([128, 4, 128]),
                                        ALU.add).then_inc(s["x_bt"][q], 1)
            for q in range(2):
                nc.gpsimd.tensor_scalar(T[q][MN], adjt[q][:, :, :], 0.0, NEG, ALU.is_le, ALU.mult)\
                  .then_inc(s["mask"][q], 1)
            for q in range(2):
                pool.wait_ge(s["ln_var"][q], i + 1)
                nc.gpsimd.tensor_tensor(small[q][:, 3, :], small[q][:, 2, :], minus_half[:, 0:4], ALU.pow)\
                  .then_inc(s["ln_rstd"][q], 1)

        body(0, True)
        with pool.Fori(1, NI) as i:
            body(i, False)

    def scalar(act, bag):
        def body(i, first):
            for q in range(2):
                act.wait_ge(s["y_act"][q], i + 1)
            for q in range(2):
                act.wait_ge(s["ln_c"][q], i + 1)
                nc.scalar.activation(T[q][SQ], T[q][H2], ACT.Square).then_inc(s["ln_sq"][q], 1)
            for q in range(2):
                act.wait_ge(s["h2_turned"][q], i + 1)
                nc.scalar.copy(T[q][H2T], bank(q, 1)).then_inc(s["h2t"][q], 1)
            for q in range(2):
                act.wait_ge(s["shifted"][q], i + 1)
                nc.scalar.activation(T[q][DEN], T[q][DEN], ACT.Exp).then_inc(s["expd"][q], 1)
            for q in range(2):
                act.wait_ge(s["min"][q], i + 1)
                nc.scalar.activation(T[q][MIN], T[q][MIN], ACT.Exp).then_inc(s["minexp"][q], 1)

        body(0, True)
        with act.Fori(1, NI) as i:
            body(i, False)

    def tensor(pe, w):
        def body(i, first):
            for q in range(2):
                pe.wait_ge(s["h_q2"][q], (i + 1) * 16)
                pe.wait_ge(s["y_leaky"][q], i + 1)
                if not first:
                    pe.wait_ge(s["out_ready"][q], i)
                for b in range(4):
                    nc.tensor.matmul(bank(q, 0)[:, b, :], T[q][H][:, b, :], w["wt1"][:, :], start=True, stop=False)
                    last = nc.tensor.matmul(bank(q, 0)[:, b, :], T[q][Y][:, b, :], w["wt2"][:, :], start=False, stop=True)
                last.then_inc(s["o_mm"][q], 1)
            for q in range(2):
                pe.wait_ge(s["h2"][q], i + 1)
                for b in range(4):
                    last = nc.tensor.transpose(bank(q, 1)[:, b, :], T[q][H2][:, b, :], w["ident"][:, :])
                last.then_inc(s["h2_turned"][q], 1)
            for q in range(2):
                pe.wait_ge(s["h2t"][q], i + 1)
                for b in range(4):
                    nc.tensor.matmul(bank(q, 1)[:, 0, b:b + 1], T[q][H2T][:, b, :], w["w2a"][:, 0:1], start=True, stop=True)
                nc.tensor.matmul(psum[:, 4 * q + 3, :], w["w1a"][:, :], T[q][H2T].rearrange("p b n -> p (b n)"),
                                 start=True, stop=True)
                for b in range(4):
                    last = nc.tensor.matmul(bank(q, 2)[:, b, :], T[q][H2T][:, b, :], w["l1w"][:, :], start=True, stop=True)
                last.then_inc(s["lin_mm"][q], 1)
            for q in range(2):
                pe.wait_ge(s["hwn"][q], i + 1)
                for b in range(4):
                    last = nc.tensor.matmul(bank(q, 0)[:, b, :], T[q][DEN][:, b, :], T[q][HWN][:, b, :], start=True, stop=True)
                last.then_inc(s["att_mm"][q], 1)

        body(0, True)
        with pe.Fori(1, NI) as i:
            body(i, False)

    def vector(dve, h_nat, bag, bn2_ready):
        dve.wait_ge(bn2_ready, 1)
        LINKS = 9

        def link(q, i, n, ins):
            ins.then_inc(s["link"][q], 1)
            dve.wait_ge(s["link"][q], i * LINKS + n)

        def body(i, first):
            for q in range(2):
                if not first:
                    dve.wait_ge(s["o_mm"][q], i)
                y = h_nat[:, bass.ds(i * 8 + 4 * q, 4), :]
                nc.vector.tensor_scalar(T[q][Y], y, bag[:, 4:5], bag[:, 6:7], ALU.mult, ALU.add).then_inc(s["y_act"][q], 1)
            for q in range(2):
                dve.wait_ge(s["y_act"][q], i + 1)
                nc.vector.scalar_tensor_tensor(T[q][Y], T[q][Y], SLOPE0, T[q][Y], ALU.mult, ALU.max).then_inc(s["y_leaky"][q], 1)
            for q in range(2):
                sm = small[q]
                dve.wait_ge(s["o_mm"][q], i + 1)
                dve.wait_ge(s["x_bt"][q], i + 1)
                nc.vector.tensor_tensor(T[q][X1], bank(q, 0), T[q][X], ALU.add).then_inc(s["x1"][q], 1)
                dve.wait_ge(s["x1"][q], i + 1)
                link(q, i, 1, nc.vector.tensor_reduce(sm[:, 0, :], T[q][X1], AX.X, ALU.add))
                link(q, i, 2, nc.vector.tensor_scalar(sm[:, 0, :], sm[:, 0, :], 1.0 / C, None, ALU.mult))
                nc.vector.tensor_tensor(T[q][H2], T[q][X1], bc(sm[:, 0, :]), ALU.subtract).then_inc(s["ln_c"][q], 1)
            for q in range(2):
                sm = small[q]
                dve.wait_ge(s["ln_sq"][q], i + 1)
                link(q, i, 3, nc.vector.tensor_reduce(sm[:, 1, :], T[q][SQ], AX.X, ALU.add))
                nc.vector.tensor_scalar(sm[:, 2, :], sm[:, 1, :], 1.0 / C, EPS, ALU.mult, ALU.add).then_inc(s["ln_var"][q], 1)
            for q in range(2):
                dve.wait_ge(s["ln_rstd"][q], i + 1)
                nc.vector.scalar_tensor_tensor(T[q][H2], T[q][H2], 0.0, bc(small[q][:, 3, :]), ALU.max, ALU.mult)\
                  .then_inc(s["h2"][q], 1)
            for q in range(2):
                sm = small[q]
                dve.wait_ge(s["lin_mm"][q], i + 1)
                dve.wait_ge(s["mask"][q], i + 1)
                link(q, i, 4, nc.vector.tensor_copy(sm[:, 4, :], bank(q, 1)[:, 0, 0:4]))
                link(q, i, 5, nc.vector.tensor_tensor(T[q][DEN], bank(q, 3), bc(sm[:, 4, :]), ALU.add))
                link(q, i, 6, nc.vector.scalar_tensor_tensor(T[q][DEN], T[q][DEN], SLOPE1, T[q][DEN], ALU.mult, ALU.max))
                nc.vector.tensor_tensor(T[q][DEN], T[q][DEN], T[q][MN], ALU.add).then_inc(s["den"][q], 1)
                dve.wait_ge(s["den"][q], i + 1)
                link(q, i, 7, nc.vector.tensor_reduce(sm[:, 5, :], T[q][DEN], AX.X, ALU.max))
                nc.vector.tensor_tensor(T[q][DEN], T[q][DEN], bc(sm[:, 5, :]), ALU.subtract).then_inc(s["shifted"][q], 1)
            for q in range(2):
                sm = small[q]
                dve.wait_ge(s["expd"][q], i + 1)
                link(q, i, 8, nc.vector.tensor_reduce(sm[:, 6, :], T[q][DEN], AX.X, ALU.add))
                link(q, i, 9, nc.vector.reciprocal(sm[:, 7, :], sm[:, 6, :]))
                nc.vector.tensor_tensor(T[q][HWN], bank(q, 2), bc(sm[:, 7, :]), ALU.mult).then_inc(s["hwn"][q], 1)
            for q in range(2):
                dve.wait_ge(s["att_mm"][q], i + 1)
                nc.vector.tensor_scalar(T[q][MIN], bank(q, 0), 0.0, None, ALU.min).then_inc(s["min"][q], 1)
            for q in range(2):
                dve.wait_ge(s["minexp"][q], i + 1)
                if not first:
                    dve.wait_ge(s["stored"][q], i * 16)
                nc.vector.scalar_tensor_tensor(T[q][OUT], bank(q, 0), 0.0, T[q][MIN], ALU.max, ALU.add).then_inc(s["y_out"][q], 1)
                dve.wait_ge(s["y_out"][q], i + 1)
                nc.vector.scalar_tensor_tensor(T[q][OUT], T[q][OUT], -1.0, T[q][X1], ALU.add, ALU.add)\
                  .then_inc(s["out_ready"][q], 1)

        body(0, True)
        with dve.Fori(1, NI) as i:
            body(i, False)

    s["y_out"] = [sem(f"f_y_out{q}") for q in range(2)]
    return dict(sync=sync, gpsimd=gpsimd, scalar=scalar, tensor=tensor, vector=vector)


def kernel(**inputs):
    import concourse.bacc as _bacc
    from concourse.bass_utils import run_bass_kernel_spmd as _run

    a = {k: np.ascontiguousarray(v) for k, v in inputs.items()}
    wt = a["L0_gnn_Wt"]
    two = lambda v: np.concatenate([v, v])
    l1a = a["L1_gnn_a"][:, 0]
    cols = np.stack([two(a["L0_gnn_g1"]), two(a["L0_gnn_be1"]), two(a["L0_gnn_b1"]), two(a["L0_gnn_W2"][0]),
                     a["L0_gnn_bg"], a["L0_gnn_gg"], a["L0_gnn_beg"], l1a[:C], l1a[C:],
                     np.broadcast_to(a["L0_gnn_b2"], (128,))], axis=1)
    node = np.arange(128)
    half = np.where(node[:, None, None] // BLK == np.arange(NBLK)[None, :, None], 0.5, 0.0)
    arrays = {
        "x": a["x"], "adj": a["adj"], "adj_t": a["adj"].transpose(0, 2, 1),
        "w1": a["L0_gnn_W1"], "w1_tt": np.concatenate([a["L0_gnn_W1"].T] * 2, axis=1),
        "wg_t": a["L0_gnn_Wg"].T, "wt1_t": wt[:, :C].T, "wt2_t": wt[:, C:].T,
        "l1_w": a["L1_gnn_W"], "l1_wt": a["L1_gnn_W"].T, "cols": cols,
        "bt_rows": np.broadcast_to(a["L0_gnn_bt"], (128, C)),
        "ident_in": np.eye(128, dtype=np.float32),
        "fold_in": (node[:, None] % MID == node[None, :] % MID).astype(np.float32),
        "half_in": np.broadcast_to(half, (128, NBLK, BLK)).astype(np.float32),
    }
    arrays = {k: np.ascontiguousarray(v) for k, v in arrays.items()}
    nc = _bacc.Bacc("TRN2", target_bir_lowering=False, num_devices=1)
    aps = [nc.dram_tensor(k, v.shape, mybir.dt.from_np(v.dtype), kind="ExternalInput").ap() for k, v in arrays.items()]
    out = nc.dram_tensor("out", (B, N, C), F32, kind="ExternalOutput").ap()
    two_layers(nc, *aps, out)
    r = _run(nc, [arrays], core_ids=[0])
    return r.results[0]["out"]
```

```python
from contextlib import ExitStack

import numpy as np

import concourse.bass as bass
from concourse import mybir

F32 = mybir.dt.float32
I32 = mybir.dt.int32
ALU = mybir.AluOpType
ACT = mybir.ActivationFunctionType
AX = mybir.AxisListType

B, N, C = 64, 128, 128
MID = 64
EPS = 1e-5
NEG = -9e15
SLOPE0, SLOPE1 = 0.01, 0.2
QUAD = 4
NQ = B // QUAD
PAIRS = float(B * N * N)

BLK = 8
NBLK = N // BLK
WIDE = 1024
BANK = 512
DIAG = 7
LAST = 8
CHUNKS = [[k, NBLK - 2 - k] for k in range(DIAG)] + [None, [DIAG]]
NCH = len(CHUNKS)
TILES = [2] * LAST + [1]
FLAT = sum(TILES) * BANK
PER = 2 * NCH
ROUNDS = 5
ROUND_END = [1, 3, 5, 7, 8]
SLOTS = 6
LAG = 2
KEEP = (0, 1, 4, 5)
KEPT = [k for k in range(PER) if k % NCH in KEEP]
PLAIN = [k for k in range(PER) if k % NCH not in KEEP]
NK, NP = len(KEPT), len(PLAIN)
ZRING = 4
NR = 2 * ROUNDS
ROUND_ENDS = [e + NCH * c for c in range(2) for e in ROUND_END]


def strip(block):
    return BLK * (block + 1), N - BLK * (block + 1)


def two_layers(nc, x, adj, adj_t, w1, w1_tt, wg_t, wt1_t, wt2_t, l1_w, l1_wt, cols, bt_rows,
               ident_in, fold_in, half_in, out):
    flat = nc.dram_tensor("score_rows", [B, FLAT], F32, kind="Internal").ap()
    kept_dram = nc.dram_tensor("kept_products", [NQ, NK, 128, 2 * BANK], F32, kind="Internal").ap()
    x_n = x.rearrange("b n c -> n b c")
    out_n = out.rearrange("b n c -> n b c")
    adj_n = adj.rearrange("b i j -> i b j")
    adj_tn = adj_t.rearrange("b j i -> j b i")

    with ExitStack() as ctx:
        def sb(name, shape, dt=F32):
            return ctx.enter_context(nc.sbuf_tensor(name, shape, dt))

        def sem(name):
            return ctx.enter_context(nc.semaphore(name))

        w1_sb = sb("w1_sb", [MID, C])
        w1tt_sb = sb("w1tt_sb", [C, 2 * MID])
        wg_sb = sb("wg_sb", [C, C])
        wt1_sb = sb("wt1_sb", [C, C])
        wt2_sb = sb("wt2_sb", [C, C])
        l1w_sb = sb("l1w_sb", [C, C])
        l1wt_sb = sb("l1wt_sb", [C, C])
        col = sb("col", [128, 10])
        G1, BE1, B1, W2, BG, GG, BEG, A1, A2, B2 = (col[:, n:n + 1] for n in range(10))
        bt_sb = sb("bt_sb", [128, C])
        ident = sb("ident", [128, 128])
        fold = sb("fold", [128, 128])
        half = sb("half", [128, NBLK, BLK])
        minus_half = sb("minus_half", [128, 16])
        ones = sb("ones", [MID, 128])
        h_nat = sb("h_nat", [N, B, C])
        h_tr = sb("h_tr", [C, B, N])
        diff = [sb(f"diff{s}", [C, 2, WIDE]) for s in range(SLOTS)]
        relu = [sb(f"relu{s}", [128, WIDE]) for s in range(SLOTS)]
        kept = [sb(f"kept{s}", [128, 2 * BANK]) for s in range(ZRING)]
        ln = sb("ln", [128, 256])
        sum_d = sb("sum_d", [128, NQ * NP])
        sum_q = sb("sum_q", [128, NQ * NP])
        kept_st = sb("kept_st", [128, NQ * NK, 2, 6])
        st = sb("st", [128, 32])
        w2_rows = sb("w2_rows", [128, 32])
        lin_rows = sb("lin_rows", [C, 2, 32])
        keep_rows = sb("keep_rows", [128, 32])
        w1a = sb("w1a", [C, 128])
        w2a = sb("w2a", [C, 128])
        s_row = [sb(f"s_row{p}", [128, ROUNDS, BANK]) for p in range(2)]
        s_up = sb("s_up", [N, QUAD, N])
        s_dg = sb("s_dg", [N, QUAD, BLK])
        s_all = sb("s_all", [N, QUAD, N])
        s_all2 = sb("s_shift", [N, QUAD, N])
        adj_sb = sb("adj_sb", [N, QUAD, N], I32)
        mneg = sb("mneg", [N, QUAD, N])
        prob = sb("prob", [N, QUAD, N])
        prob_tr = sb("prob_tr", [N, QUAD, N])
        h_q = sb("h_q", [N, QUAD, C])
        mix = sb("mix", [C, QUAD, N])
        rows = sb("rows", [N, 3, QUAD])
        bst = sb("bst", [C, NQ, 6])
        bag = sb("bag", [C, 8])

        psum = ctx.enter_context(nc.psum_tensor("psum", [128, 8, BANK], F32))
        prod = [psum[:, 2 * n:2 * n + 2, :] for n in range(3)]
        score = [psum[:, 6, :], psum[:, 7, :]]
        att = [psum[:, 4, :].rearrange("p (b n) -> p b n", b=QUAD),
               psum[:, 5, :].rearrange("p (b n) -> p b n", b=QUAD)]

        weights_in = sem("weights_in")
        x_in = [sem(f"x_in{g}") for g in range(4)]
        dve_ln = sem("dve_ln")
        centred = sem("centred")
        squared = sem("squared")
        var_ready = sem("var_ready")
        rstd_ready = sem("rstd_ready")
        h_ready = sem("h_ready")
        turned = sem("turned")
        h_tr_ready = sem("h_tr_ready")
        consts_set = sem("consts_set")
        wa_mm = sem("wa_mm")
        wa_ready = sem("wa_ready")

        diff_ready = [sem("diff_ready1"), sem("diff_ready2")]
        abs_ready = [sem("abs_ready1"), sem("abs_ready2")]
        prod_ready = [sem("prod_ready1"), sem("prod_ready2")]
        prod_free = sem("prod_free")
        kept_counted = sem("kept_counted")
        kept_stored = [sem(f"kept_stored{s}") for s in range(ZRING)]
        kept_in = [sem(f"kept_in{s}") for s in range(ZRING)]
        lin_done = sem("lin_done")
        relu_ready = sem("relu_ready")
        shift_mm = sem("shift_mm")
        shift_ready = sem("shift_ready")
        stat = sem("stat")
        stat_sums = sem("stat_sums")
        stat_mm = sem("stat_mm")
        stat_var = sem("stat_var")
        stat_rstd = sem("stat_rstd")
        stat_lin = sem("stat_lin")
        stat_lin_mm = sem("stat_lin_mm")
        pass2_ready = sem("pass2_ready")
        round_done = sem("round_done")
        row_ready = sem("row_ready")
        rows_stored = [sem("rows_stored0"), sem("rows_stored1")]
        s_up_clear = sem("s_up_clear")
        s_in = sem("s_in")
        adj_in = sem("adj_in")
        hq_in = sem("hq_in")
        diag_set = sem("diag_set")
        s_half_ready = sem("s_half_ready")
        mask_ready = sem("mask_ready")
        s_sum = sem("s_sum")
        s_masked = sem("s_masked")
        dve_att = sem("dve_att")
        s_shifted = sem("s_shifted")
        exp_done = sem("exp_done")
        prob_ready = sem("prob_ready")
        prob_turned = sem("prob_turned")
        prob_tr_ready = sem("prob_tr_ready")
        mixed = sem("mixed")
        mix_ready = sem("mix_ready")
        y_mm = sem("y_mm")
        y_ready = sem("y_ready")
        bn2 = sem("bn2")
        bn2_var = sem("bn2_var")
        bn2_rstd = sem("bn2_rstd")
        bn2_ready = sem("bn2_ready")

        final = final_tiles(nc, sb, sem, diff, relu, psum)

        block = ctx.enter_context(nc.Block())

        def sc(n):
            return st[:, n:n + 1]

        def chunk_at(i, k):
            return i * PER + k

        def ln_sum(g):
            return ln[:, 16 * g:16 * g + 16]

        def ln_sq(g):
            return ln[:, 64 + 16 * g:80 + 16 * g]

        def ln_var(g):
            return ln[:, 128 + 16 * g:144 + 16 * g]

        def ln_rstd(g):
            return ln[:, 192 + 16 * g:208 + 16 * g]

        def group(g):
            return h_nat[:, 16 * g:16 * g + 16, :]

        def sq_tile(g):
            return diff[g][:, :, :].rearrange("p a (b c) -> p (a b) c", c=C)

        def bcast(v, n):
            return v.unsqueeze(2).broadcast_to([v.shape[0], v.shape[1], n])

        def tr_tile(g):
            return psum[:, 4 * (g % 2):4 * (g % 2) + 4, :]

        def diff_place(phase, i, k):
            if phase == 0:
                return chunk_at(i, k), k % SLOTS
            p = PLAIN.index(k)
            return i * NP + p, p % (NP // 2)

        def rounds_before(i, k):
            back = 0
            if k < 0:
                k += PER
                back = 1
            return (i - back) * NR + next(n for n, e in enumerate(ROUND_ENDS) if k <= e) + 1

        def ended(i, k, lag, depth):
            m = k - lag
            if m >= 0:
                return [(i, ROUND_ENDS.index(m))] if m in ROUND_ENDS else []
            return [(i - 1, ROUND_ENDS.index(m + PER))] if depth > 0 and m + PER in ROUND_ENDS else []

        def att_steps(table, i, k, depth):
            found = []
            if k in table and depth > 0:
                found.append((table[k], i - 1))
            if k + PER in table and depth > 1:
                found.append((table[k + PER], i - 2))
            return found

        def att_rest(table):
            return [(table[p], NQ - 2) for p in sorted(table) if p >= PER] + [(table[p], NQ - 1) for p in sorted(table)]

        @block.sync
        def _(sp):
            for g in range(4):
                sp.dma_start(h_nat[:, 16 * g:16 * g + 16, :], x_n[:, 16 * g:16 * g + 16, :]).then_inc(x_in[g], 16)

            def store_rows(i, c):
                sp.wait_ge(row_ready, (i * 2 + c + 1) * ROUNDS)
                for g in range(2):
                    dst = flat[bass.ds(i * QUAD + 2 * c + g, 1), :]
                    for q in range(4):
                        sp.dma_start(dst[:, 0:16 * BANK].rearrange("b (r q x) -> b r q x", q=4, x=BANK)[:, :, q, :],
                                     s_row[c][32 * q + g:32 * q + g + 1, 0:4, :]).then_inc(rows_stored[c], 16)
                    sp.dma_start(dst[:, 16 * BANK:FLAT],
                                 s_row[c][g:g + 1, 4, :]).then_inc(rows_stored[c], 16)

            def load_scores(i, first):
                for c in range(2):
                    sp.wait_ge(rows_stored[c], (i + 1) * 10 * 16)
                if not first:
                    sp.wait_ge(s_half_ready, i)
                else:
                    sp.wait_ge(s_up_clear, 1)
                src = flat[bass.ds(i * QUAD, QUAD), :]
                for k, blocks in enumerate(CHUNKS):
                    at = k * WIDE
                    if blocks is None:
                        sp.dma_start(s_dg[:, :, :], src[:, at:at + WIDE].rearrange("b (p j) -> p b j", j=BLK))\
                          .then_inc(s_in, 16)
                        continue
                    for blk in blocks:
                        j0, n = strip(blk)
                        sp.dma_start(s_up[BLK * blk:BLK * blk + BLK, :, j0:N],
                                     src[:, at:at + BLK * n].rearrange("b (p j) -> p b j", j=n))\
                          .then_inc(s_in, 16)
                        at += BLK * n

            def load_graphs(i, first):
                if not first:
                    sp.wait_ge(mask_ready, i)
                    sp.wait_ge(mixed, i)
                sp.dma_start(adj_sb[:, :, :], adj_n[:, bass.ds(i * QUAD, QUAD), :]).then_inc(adj_in, 16)
                sp.dma_start(h_q[:, :, :], h_nat[:, bass.ds(i * QUAD, QUAD), :]).then_inc(hq_in, 16)

            def store_kept(i):
                for n in range(NK):
                    sp.wait_ge(prod_free, chunk_at(i, KEPT[n]) + 1)
                    sp.dma_start(kept_dram[bass.ds(i, 1), n, :, :].rearrange("a p x -> p (a x)"),
                                 kept[n % ZRING][:, :]).then_inc(kept_stored[n % ZRING], 16)

            store_kept(0)
            with sp.Fori(1, NQ) as i:
                store_kept(i)
            for z in range(ZRING):
                sp.wait_ge(kept_stored[z], NQ * NK // ZRING * 16)
            sp.wait_ge(kept_counted, NQ * NK)

            def load_kept(i, n, depth):
                if depth > 0 or n >= ZRING:
                    back, m = (0, n - ZRING) if n >= ZRING else (1, n - ZRING + NK)
                    sp.wait_ge(round_done, rounds_before(i - back, KEPT[m]))
                sp.dma_start(kept[n % ZRING][:, :],
                             kept_dram[bass.ds(i, 1), n, :, :].rearrange("a p x -> p (a x)"))\
                  .then_inc(kept_in[n % ZRING], 16)

            def graphs(i, depth):
                for n in range(NK):
                    if n == 2 and depth > 0:
                        store_rows(i - 1, 0)
                    if n == 6 and depth > 0:
                        store_rows(i - 1, 1)
                        load_graphs(i - 1, depth == 1)
                        load_scores(i - 1, depth == 1)
                    load_kept(i, n, depth)

            graphs(0, 0)
            graphs(1, 1)
            with sp.Fori(2, NQ) as i:
                graphs(i, 2)
            store_rows(NQ - 1, 0)
            store_rows(NQ - 1, 1)
            load_graphs(NQ - 1, False)
            load_scores(NQ - 1, False)
            final["sync"](sp, x_n, out_n, adj_tn, h_nat, h_tr, y_ready)

        @block.gpsimd
        def _(pool):
            nc.gpsimd.memset(minus_half[:, :], -0.5)
            nc.gpsimd.memset(ones[:, :], 1.0)
            nc.gpsimd.memset(w2_rows[:, :], 0.0)
            nc.gpsimd.memset(keep_rows[:, :], 0.0)
            nc.gpsimd.memset(lin_rows[:, :, :], 0.0).then_inc(consts_set, 1)
            nc.gpsimd.memset(s_up[:, :, :], 0.0).then_inc(s_up_clear, 1)
            pool.wait_ge(consts_set, 1)
            for g in range(4):
                pool.wait_ge(var_ready, g + 1)
                nc.gpsimd.tensor_tensor(ln_rstd(g), ln_var(g), minus_half[:, 0:16], ALU.pow).then_inc(rstd_ready, 1)
            pool.wait_ge(stat_var, 1)
            nc.gpsimd.tensor_tensor(sc(11), sc(10), minus_half[:, 0:1], ALU.pow).then_inc(stat_rstd, 1)

            def assemble(i):
                pool.wait_ge(weights_in, 16 * 12)
                pool.wait_ge(s_in, (i + 1) * 16 * 16)
                if not isinstance(i, int) or i > 0:
                    pool.wait_ge(s_sum, i)
                nc.gpsimd.tensor_tensor(s_all[:, :, :].rearrange("p b (k j) -> p b k j", j=BLK),
                                        s_dg[:, :, :].unsqueeze(2).broadcast_to([N, QUAD, NBLK, BLK]),
                                        half[:, :, :].unsqueeze(1).broadcast_to([N, QUAD, NBLK, BLK]),
                                        ALU.mult).then_inc(diag_set, 1)
                pool.wait_ge(adj_in, (i + 1) * 16)
                if not isinstance(i, int) or i > 0:
                    pool.wait_ge(s_masked, i)
                pool.wait_ge(diag_set, i + 1)
                nc.gpsimd.tensor_tensor(s_all[:, :, :], s_all[:, :, :], s_up[:, :, :], ALU.add)\
                  .then_inc(s_half_ready, 1)
                nc.gpsimd.tensor_scalar(mneg[:, :, :], adj_sb[:, :, :], 0.0, NEG, ALU.is_le, ALU.mult)\
                  .then_inc(mask_ready, 1)

            assemble(0)
            with pool.Fori(1, NQ) as i:
                assemble(i)
            pool.wait_ge(bn2_var, 1)
            nc.gpsimd.tensor_tensor(bag[:, 3:4], bag[:, 2:3], minus_half[:, 0:1], ALU.pow).then_inc(bn2_rstd, 1)
            final["gpsimd"](pool, bt_sb, minus_half)

        @block.scalar
        def _(act):
            for t, src in ((w1_sb, w1), (w1tt_sb, w1_tt), (wg_sb, wg_t), (wt1_sb, wt1_t), (wt2_sb, wt2_t),
                           (l1w_sb, l1_w), (l1wt_sb, l1_wt), (col, cols), (bt_sb, bt_rows),
                           (ident, ident_in), (fold, fold_in)):
                act.dma_start(t[:, :], src).then_inc(weights_in, 16)
            act.dma_start(half[:, :, :], half_in).then_inc(weights_in, 16)
            for g in range(4):
                act.wait_ge(centred, g + 1)
                nc.scalar.activation(sq_tile(g), group(g), ACT.Square).then_inc(squared, 1)
                if g > 0:
                    act.wait_ge(turned, g)
                    nc.scalar.copy(h_tr[:, 16 * g - 16:16 * g, :], tr_tile(g - 1)).then_inc(h_tr_ready, 1)
            act.wait_ge(turned, 4)
            nc.scalar.copy(h_tr[:, 48:64, :], tr_tile(3)).then_inc(h_tr_ready, 1)

            def absolute(phase, i, k):
                n = WIDE if k % NCH != LAST else BANK
                at, slot = diff_place(phase, i, k)
                act.wait_ge(diff_ready[phase], at + 1)
                tile = diff[slot][:, :, 0:n]
                acc = sum_d[:, bass.ds(i * NP + PLAIN.index(k), 1)] if phase == 0 and k in PLAIN else None
                nc.scalar.activation(tile, tile, ACT.Abs, accum_out=acc).then_inc(abs_ready[phase], 1)

            def take(i, k, depth):
                t = TILES[k % NCH]
                act.wait_ge(prod_ready[0], chunk_at(i, k) + 1)
                tile = prod[k % 3][:, 0:t, :]
                if k in PLAIN:
                    nc.scalar.activation(tile, tile, ACT.Square, bias=sc(0),
                                         accum_out=sum_q[:, bass.ds(i * NP + PLAIN.index(k), 1)]).then_inc(prod_free, 1)
                    return
                n = KEPT.index(k)
                if depth > 0 or n >= ZRING:
                    act.wait_ge(kept_counted, i * NK + n - ZRING + 1)
                    act.wait_ge(kept_stored[n % ZRING], (i * (NK // ZRING) + n // ZRING) * 16)
                nc.scalar.copy(kept[n % ZRING][:, :], tile.rearrange("p a b -> p (a b)")).then_inc(prod_free, 1)

            def pass1_body(i, first):
                for k in range(PER):
                    absolute(0, i, k)
                    if k > 0:
                        if first and k - 1 == PLAIN[0]:
                            act.wait_ge(shift_ready, 1)
                        take(i, k - 1, 0 if first else 1)
                    elif not first:
                        take(i - 1, PER - 1, 1)

            pass1_body(0, True)
            with act.Fori(1, NQ) as i:
                pass1_body(i, False)
            take(NQ - 1, PER - 1, 1)

            def rectify(i, k, depth):
                t = TILES[k % NCH]
                if depth > 0 or k >= SLOTS:
                    act.wait_ge(round_done, rounds_before(i, k - SLOTS))
                if k in PLAIN:
                    p = PLAIN.index(k)
                    act.wait_ge(prod_ready[1], i * NP + p + 1)
                    src = prod[p % 2][:, 0:t, :].rearrange("p a b -> p (a b)")
                else:
                    n = KEPT.index(k)
                    act.wait_ge(kept_in[n % ZRING], (i * (NK // ZRING) + n // ZRING + 1) * 16)
                    src = kept[n % ZRING][:, :]
                nc.scalar.activation(relu[k % SLOTS][:, 0:t * BANK], src, ACT.Relu, bias=sc(14), scale=sc(12))\
                  .then_inc(relu_ready, 1)

            def exps(i):
                act.wait_ge(s_shifted, i + 1)
                nc.scalar.activation(prob[:, :, :], s_all2[:, :, :], ACT.Exp).then_inc(exp_done, 1)

            def pass2_body(i, depth):
                for k in range(PER):
                    if k in PLAIN:
                        absolute(1, i, k)
                    if k > 0:
                        rectify(i, k - 1, depth)
                    elif depth > 0:
                        rectify(i - 1, PER - 1, depth - 1)
                    for step, j in att_steps({16: exps}, i, k, depth):
                        step(j)

            act.wait_ge(pass2_ready, 1)
            pass2_body(0, 0)
            pass2_body(1, 1)
            with act.Fori(2, NQ) as i:
                pass2_body(i, 2)
            rectify(NQ - 1, PER - 1, 2)
            exps(NQ - 1)
            act.wait_ge(bn2_ready, 1)
            final["scalar"](act, bag, h_nat, h_tr)

        @block.tensor
        def _(pe):
            pe.wait_ge(weights_in, 16 * 12)
            nc.tensor.matmul(psum[:, 0, 0:1], l1wt_sb[:, :], A1, start=True, stop=True)
            nc.tensor.matmul(psum[:, 0, 1:2], l1wt_sb[:, :], A2, start=True, stop=True).then_inc(wa_mm, 1)
            pe.wait_ge(wa_ready, 1)
            for g in range(4):
                pe.wait_ge(h_ready, g + 1)
                if g >= 2:
                    pe.wait_ge(h_tr_ready, g - 1)
                for b in range(16):
                    last = nc.tensor.transpose(tr_tile(g)[:, b // 4, 128 * (b % 4):128 * (b % 4) + 128],
                                               h_nat[:, 16 * g + b, :], ident[:, :])
                last.then_inc(turned, 1)
            pe.wait_ge(h_tr_ready, 4)

            def products(phase, i, k):
                at, slot = diff_place(phase, i, k)
                n = k % 3 if phase == 0 else PLAIN.index(k) % 2
                pe.wait_ge(abs_ready[phase], at + 1)
                for t in range(TILES[k % NCH]):
                    for g in range(2):
                        last = nc.tensor.matmul(prod[n][MID * g:MID * g + MID, t, :], w1tt_sb[:, 0:MID],
                                                diff[slot][:, g, t * BANK:t * BANK + BANK],
                                                start=True, stop=True)
                last.then_inc(prod_ready[phase], 1)

            def pass1_body(i, first):
                for k in range(PER):
                    if not (first and k < 3):
                        pe.wait_ge(prod_free, chunk_at(i, k) - 2)
                    products(0, i, k)
                    if first and k == PLAIN[0]:
                        nc.tensor.matmul(score[0][:, 0:1], w1tt_sb[:, :], sum_d[:, 0:1],
                                         start=True, stop=True).then_inc(shift_mm, 1)

            pass1_body(0, True)
            with pe.Fori(1, NQ) as i:
                pass1_body(i, False)

            pe.wait_ge(stat_sums, 1)
            nc.tensor.matmul(score[0][:, 1:2], w1tt_sb[:, :], sc(3), start=True, stop=False)
            nc.tensor.matmul(score[0][:, 1:2], fold[:, :], sc(22), start=False, stop=True)
            nc.tensor.matmul(score[0][:, 2:3], fold[:, :], sc(6), start=True, stop=True).then_inc(stat_mm, 1)
            pe.wait_ge(stat_lin, 1)
            nc.tensor.matmul(score[0][:, 3:4], w1_sb[:, :], st[0:MID, 16:17], start=True, stop=True)
            nc.tensor.matmul(score[0][:, 4:5], ones[:, :], st[0:MID, 17:18], start=True, stop=True).then_inc(stat_lin_mm, 1)
            pe.wait_ge(pass2_ready, 1)

            def parts(done):
                c, r = divmod(done, ROUNDS)
                return [(q, c * NCH + (4 * r + q) // 2, q % 2) for q in range(4 if r < ROUNDS - 1 else 1)]

            def slopes(i, done, depth):
                if depth > 0 or done >= 2:
                    pe.wait_ge(row_ready, i * NR + done - 1)
                bank = score[done % 2]
                tiles = parts(done)
                if tiles[0][1] in KEPT:
                    for q, k, t in tiles:
                        n = KEPT.index(k)
                        if t == 0:
                            pe.wait_ge(kept_in[n % ZRING], (i * (NK // ZRING) + n // ZRING + 1) * 16)
                        last = nc.tensor.matmul(bank[32 * q:32 * q + 32, :], keep_rows[:, :],
                                                kept[n % ZRING][:, t * BANK:t * BANK + BANK], start=True, stop=False)
                else:
                    for g in range(2):
                        for q, k, t in tiles:
                            slot = diff_place(1, 0, k)[1]
                            last = nc.tensor.matmul(bank[32 * q:32 * q + 32, :], lin_rows[:, g, :],
                                                    diff[slot][:, g, t * BANK:t * BANK + BANK],
                                                    start=(g == 0), stop=False)
                last.then_inc(lin_done, 1)

            def scores(i, done):
                pe.wait_ge(relu_ready, chunk_at(i, ROUND_ENDS[done]) + 1)
                for q, k, t in parts(done):
                    last = nc.tensor.matmul(score[done % 2][32 * q:32 * q + 32, :], w2_rows[:, :],
                                            relu[k % SLOTS][:, t * BANK:t * BANK + BANK], start=False, stop=True)
                last.then_inc(round_done, 1)

            def att_sum(i):
                pe.wait_ge(s_half_ready, i + 1)
                for b in range(QUAD):
                    nc.tensor.matmul(att[0][:, b, :], ident[:, :], s_all[:, b, :], start=True, stop=False)
                    last = nc.tensor.matmul(att[0][:, b, :], s_all[:, b, :], ident[:, :], start=False, stop=True)
                last.then_inc(s_sum, 1)

            def att_turn(i):
                pe.wait_ge(prob_ready, i + 1)
                for b in range(QUAD):
                    last = nc.tensor.transpose(att[1][:, b, :], prob[:, b, :], ident[:, :])
                last.then_inc(prob_turned, 1)

            def att_mix(i):
                pe.wait_ge(prob_tr_ready, i + 1)
                pe.wait_ge(hq_in, (i + 1) * 16)
                for b in range(QUAD):
                    last = nc.tensor.matmul(att[0][:, b, :], h_q[:, b, :], prob_tr[:, b, :], start=True, stop=True)
                last.then_inc(mixed, 1)

            def att_out(i):
                pe.wait_ge(mix_ready, i + 1)
                nc.tensor.matmul(psum[:, 5, :], wg_sb[:, :], mix[:, :, :].rearrange("p b n -> p (b n)"),
                                 start=True, stop=True).then_inc(y_mm, 1)

            ATT = {13: att_sum, 18: att_turn, 20: att_mix, 22: att_out}

            def pass2_body(i, depth):
                for k in range(PER):
                    if k in PLAIN:
                        p = PLAIN.index(k)
                        if depth > 0 or p >= 2:
                            back, m = (0, p - 2) if p >= 2 else (1, p - 2 + NP)
                            pe.wait_ge(relu_ready, chunk_at(i - back, PLAIN[m]) + 1)
                        products(1, i, k)
                    for j, done in ended(i, k, LAG, depth):
                        scores(j, done)
                    for j, done in ended(i, k, 0, depth):
                        slopes(j, done, depth)
                    for step, j in att_steps(ATT, i, k, depth):
                        step(j)

            pass2_body(0, 0)
            pass2_body(1, 1)
            with pe.Fori(2, NQ) as i:
                pass2_body(i, 2)
            for k in range(LAG):
                for j, done in ended(NQ, k, LAG, 2):
                    scores(j, done)
            for step, j in att_rest(ATT):
                step(j)
            final["tensor"](pe, wt1_sb, wt2_sb, l1w_sb, w1a, w2a, ident)

        @block.vector
        def _(dve):
            count = [0]

            def ln_step(ins):
                count[0] += 1
                ins.then_inc(dve_ln, 1)
                return count[0]

            def centre(g):
                dve.wait_ge(x_in[g], 16)
                dve.wait_ge(dve_ln, ln_step(nc.vector.tensor_reduce(ln_sum(g), group(g), AX.X, ALU.add)))
                dve.wait_ge(dve_ln, ln_step(nc.vector.tensor_scalar(ln_sum(g), ln_sum(g), 1.0 / C, None, ALU.mult)))
                nc.vector.tensor_tensor(group(g), group(g), bcast(ln_sum(g), C), ALU.subtract).then_inc(centred, 1)

            def scale(g):
                dve.wait_ge(squared, g + 1)
                dve.wait_ge(dve_ln, ln_step(nc.vector.tensor_reduce(ln_sq(g), sq_tile(g), AX.X, ALU.add)))
                nc.vector.tensor_scalar(ln_var(g), ln_sq(g), 1.0 / C, EPS, ALU.mult, ALU.add).then_inc(var_ready, 1)
                dve.wait_ge(rstd_ready, g + 1)
                nc.vector.scalar_tensor_tensor(group(g), group(g), 0.0, bcast(ln_rstd(g), C), ALU.max, ALU.mult)\
                  .then_inc(h_ready, 1)

            dve.wait_ge(wa_mm, 1)
            dve.wait_ge(weights_in, 16 * 12)
            nc.vector.tensor_copy(w1a[:, :], psum[:, 0, 0:1].broadcast_to([C, 128]))
            nc.vector.tensor_copy(w2a[:, :], psum[:, 0, 1:2].broadcast_to([C, 128])).then_inc(wa_ready, 1)
            centre(0)
            for g in range(4):
                if g < 3:
                    centre(g + 1)
                scale(g)
            dve.wait_ge(h_tr_ready, 4)

            def differences(phase, i, k, depth):
                at, slot = diff_place(phase, i, k)
                if phase == 0 and (depth > 0 or k >= SLOTS):
                    dve.wait_ge(prod_ready[0], at - SLOTS + 1)
                elif phase == 1 and (depth > 0 or k >= NCH):
                    dve.wait_ge(lin_done, rounds_before(i, k - NCH))
                c, m = divmod(k, NCH)
                tile = diff[slot]
                two = h_tr[:, bass.ds(i * QUAD + 2 * c, 2), :]
                if CHUNKS[m] is None:
                    for g in range(2):
                        one = h_tr[:, bass.ds(i * QUAD + 2 * c + g, 1), :].rearrange("p a (k j) -> p (a k) j", j=BLK)
                        last = nc.vector.tensor_tensor(
                            tile[:, g, :].rearrange("p (k i j) -> p k i j", i=BLK, j=BLK),
                            one.unsqueeze(2).broadcast_to([C, NBLK, BLK, BLK]),
                            one.unsqueeze(3).broadcast_to([C, NBLK, BLK, BLK]), ALU.subtract)
                    last.then_inc(diff_ready[phase], 1)
                    return
                at = 0
                for blk in CHUNKS[m]:
                    j0, n = strip(blk)
                    last = nc.vector.tensor_tensor(
                        tile[:, :, at:at + BLK * n].rearrange("p a (i j) -> p a i j", j=n),
                        two[:, :, j0:N].unsqueeze(2).broadcast_to([C, 2, BLK, n]),
                        two[:, :, j0 - BLK:j0].unsqueeze(3).broadcast_to([C, 2, BLK, n]), ALU.subtract)
                    at += BLK * n
                last.then_inc(diff_ready[phase], 1)

            def count_kept(i, k):
                n = KEPT.index(k)
                dve.wait_ge(prod_free, chunk_at(i, k) + 1)
                for t in range(2):
                    last = nc.vector.bn_stats(kept_st[:, bass.ds(i * NK + n, 1), t, :].rearrange("p a s -> p (a s)"),
                                              kept[n % ZRING][:, t * BANK:t * BANK + BANK])
                last.then_inc(kept_counted, 1)

            def pass1_body(i, first):
                for k in range(PER):
                    differences(0, i, k, 0 if first else 1)
                    if k - 3 in KEPT:
                        count_kept(i, k - 3)
                    if first and k == PLAIN[0] + 2:
                        dve.wait_ge(shift_mm, 1)
                        nc.vector.tensor_scalar(sc(0), score[0][:, 0:1], -0.5 / WIDE, None, ALU.mult)\
                          .then_inc(shift_ready, 1)

            pass1_body(0, True)
            with dve.Fori(1, NQ) as i:
                pass1_body(i, False)

            done = [0]

            def then(ins):
                done[0] += 1
                ins.then_inc(stat, 1)
                dve.wait_ge(stat, done[0])

            dve.wait_ge(prod_free, NQ * PER)
            dve.wait_ge(kept_counted, NQ * NK)
            v_d = sum_d[:, :].rearrange("p (q k) -> p q k", k=NP // 2)[:, :, PLAIN.index(DIAG)]
            v_q = sum_q[:, :].rearrange("p (q k) -> p q k", k=NP // 2)[:, :, PLAIN.index(DIAG)]
            nc.vector.tensor_reduce(sc(1), sum_d[:, :], AX.X, ALU.add)
            nc.vector.tensor_reduce(sc(2), v_d, AX.X, ALU.add)
            nc.vector.tensor_reduce(sc(4), sum_q[:, :], AX.X, ALU.add)
            then(nc.vector.tensor_reduce(sc(5), v_q, AX.X, ALU.add))
            nc.vector.scalar_tensor_tensor(sc(3), sc(1), 2.0, sc(2), ALU.mult, ALU.subtract)
            then(nc.vector.scalar_tensor_tensor(sc(6), sc(4), 2.0, sc(5), ALU.mult, ALU.subtract))
            kept_n = float(2 * NQ * NK * 2 * BANK)
            then(nc.vector.bn_aggr(st[:, 20:22], kept_st[:, :, :, :].rearrange("p n t s -> p (n t s)")))
            nc.vector.tensor_scalar(sc(22), sc(20), kept_n, None, ALU.mult)
            then(nc.vector.tensor_tensor(sc(23), sc(20), sc(0), ALU.add))
            then(nc.vector.tensor_tensor(sc(23), sc(23), sc(23), ALU.mult))
            then(nc.vector.tensor_tensor(sc(23), sc(23), sc(21), ALU.add))
            nc.vector.scalar_tensor_tensor(sc(6), sc(23), kept_n, sc(6), ALU.mult, ALU.add).then_inc(stat_sums, 1)
            dve.wait_ge(stat_mm, 1)
            then(nc.vector.tensor_scalar(sc(7), score[0][:, 1:2], 1.0 / PAIRS, None, ALU.mult))
            then(nc.vector.tensor_tensor(sc(8), sc(7), sc(0), ALU.add))
            then(nc.vector.tensor_tensor(sc(9), sc(8), sc(8), ALU.mult))
            then(nc.vector.scalar_tensor_tensor(sc(9), score[0][:, 2:3], 1.0 / PAIRS, sc(9), ALU.mult, ALU.subtract))
            nc.vector.tensor_scalar(sc(10), sc(9), EPS, None, ALU.add).then_inc(stat_var, 1)
            dve.wait_ge(stat_rstd, 1)
            then(nc.vector.tensor_tensor(sc(12), sc(11), G1, ALU.mult))
            then(nc.vector.tensor_tensor(sc(13), sc(7), B1, ALU.add))
            then(nc.vector.tensor_tensor(sc(13), B1, sc(13), ALU.subtract))
            then(nc.vector.tensor_tensor(sc(14), sc(13), sc(12), ALU.mult))
            then(nc.vector.tensor_tensor(sc(14), sc(14), BE1, ALU.add))
            then(nc.vector.tensor_scalar(sc(15), W2, SLOPE0, None, ALU.mult))
            then(nc.vector.tensor_tensor(sc(16), sc(15), sc(12), ALU.mult))
            nc.vector.tensor_tensor(sc(17), sc(15), sc(14), ALU.mult).then_inc(stat_lin, 1)
            for g in range(2):
                part = slice(MID * g, MID * g + MID)
                nc.vector.tensor_scalar(w2_rows[part, g:g + 1], col[part, 3:4], 1.0 - SLOPE0, None, ALU.mult)
                nc.vector.tensor_copy(keep_rows[part, g:g + 1], st[part, 16:17])
            dve.wait_ge(stat_lin_mm, 1)
            for g in range(2):
                nc.vector.tensor_copy(lin_rows[:, g, g:g + 1], score[0][:, 3:4])
            nc.vector.tensor_tensor(sc(18), score[0][:, 4:5], B2, ALU.add).then_inc(pass2_ready, 1)
            dve.wait_ge(pass2_ready, 1)

            def evacuate(i, done, depth):
                c, r = divmod(done, ROUNDS)
                dve.wait_ge(round_done, i * NR + done + 1)
                if depth > 0:
                    dve.wait_ge(rows_stored[c], i * 160)
                p = 128 if r < ROUNDS - 1 else 32
                nc.vector.tensor_copy(s_row[c][0:p, r, :], score[done % 2][0:p, :]).then_inc(row_ready, 1)

            def link(i, n, ins):
                ins.then_inc(dve_att, 1)
                dve.wait_ge(dve_att, i * 4 + n)

            def att_scores(i):
                dve.wait_ge(s_sum, i + 1)
                dve.wait_ge(mask_ready, i + 1)
                nc.vector.scalar_tensor_tensor(s_all2[:, :, :], att[0], sc(18), mneg[:, :, :], ALU.add, ALU.add)\
                  .then_inc(s_masked, 1)
                dve.wait_ge(s_masked, i + 1)
                link(i, 1, nc.vector.tensor_reduce(rows[:, 0, :], s_all2[:, :, :], AX.X, ALU.max))
                nc.vector.tensor_tensor(s_all2[:, :, :], s_all2[:, :, :], bcast(rows[:, 0, :], N), ALU.subtract)\
                  .then_inc(s_shifted, 1)

            def att_norm(i):
                dve.wait_ge(exp_done, i + 1)
                link(i, 2, nc.vector.tensor_reduce(rows[:, 1, :], prob[:, :, :], AX.X, ALU.add))
                link(i, 3, nc.vector.reciprocal(rows[:, 2, :], rows[:, 1, :]))
                nc.vector.tensor_tensor(prob[:, :, :], prob[:, :, :], bcast(rows[:, 2, :], N), ALU.mult)\
                  .then_inc(prob_ready, 1)

            def att_copy(i):
                dve.wait_ge(prob_turned, i + 1)
                nc.vector.tensor_copy(prob_tr[:, :, :], att[1]).then_inc(prob_tr_ready, 1)

            def att_mix(i):
                dve.wait_ge(mixed, i + 1)
                nc.vector.tensor_copy(mix[:, :, :], att[0]).then_inc(mix_ready, 1)

            def att_y(i):
                dve.wait_ge(y_mm, i + 1)
                y = h_nat[:, bass.ds(i * QUAD, QUAD), :]
                link(i, 4, nc.vector.tensor_scalar(y, att[1], BG, None, ALU.add))
                nc.vector.bn_stats(bst[:, bass.ds(i, 1), :].rearrange("p a s -> p (a s)"),
                                   y.rearrange("p b n -> p (b n)")).then_inc(y_ready, 1)

            ATT = {17: att_scores, 20: att_norm, 22: att_copy, 24: att_mix, 26: att_y}
            AHEAD = 3

            def pass2_body(i, depth):
                for k in range(PER):
                    if k in PLAIN:
                        differences(1, i, k, depth)
                    for j, done in ended(i, k, LAG + AHEAD, depth):
                        evacuate(j, done, depth if k >= LAG + AHEAD else depth - 1)
                    for step, j in att_steps(ATT, i, k, depth):
                        step(j)

            pass2_body(0, 0)
            pass2_body(1, 1)
            with dve.Fori(2, NQ) as i:
                pass2_body(i, 2)
            for k in range(LAG + AHEAD):
                for j, done in ended(NQ, k, LAG + AHEAD, 2):
                    evacuate(j, done, 2)
            for step, j in att_rest(ATT):
                step(j)

            def then2(n, ins):
                ins.then_inc(bn2, 1)
                dve.wait_ge(bn2, n)

            dve.wait_ge(y_ready, NQ)
            then2(1, nc.vector.bn_aggr(bag[:, 0:2], bst[:, :, :].rearrange("p q s -> p (q s)")))
            nc.vector.tensor_scalar(bag[:, 2:3], bag[:, 1:2], EPS, None, ALU.add).then_inc(bn2_var, 1)
            dve.wait_ge(bn2_rstd, 1)
            then2(2, nc.vector.tensor_tensor(bag[:, 4:5], bag[:, 3:4], GG, ALU.mult))
            then2(3, nc.vector.tensor_tensor(bag[:, 5:6], bag[:, 0:1], bag[:, 4:5], ALU.mult))
            nc.vector.tensor_tensor(bag[:, 6:7], BEG, bag[:, 5:6], ALU.subtract).then_inc(bn2_ready, 1)
            final["vector"](dve, h_nat, bn2_ready)


def final_tiles(nc, sb, sem, diff, relu, psum):
    NS = 4
    NI = B // (4 * NS)
    store = [t[:, n // 2, BANK * (n % 2):BANK * (n % 2) + BANK] for t in diff for n in range(4)] + \
            [t[:, BANK * n:BANK * n + BANK] for t in relu for n in range(2)]
    store = [t.rearrange("p (b n) -> p b n", b=4) for t in store]
    X, H, Y, CEN, SQ, X1, HT = (store[NS * n:NS * n + NS] for n in range(7))
    H2T, MASK, DEN, HWN, MIN, OUT = (store[NS * n:NS * n + NS] for n in range(6))
    adjt = [t.bitcast(I32) for t in store[NS * 6:NS * 7]]
    small = sb("small", [128, NS, 6, 4])
    bank = [[psum[:, 2 * q + n, :].rearrange("p (b n) -> p b n", b=4) for n in range(2)] for q in range(NS)]

    x_in2, h_in2, x1_kept, h2_kept, h2_in, adjt_in, out_stored = (
        [sem(f"{n}{q}") for q in range(NS)]
        for n in ("x_in2_", "h_in2_", "x1_kept", "h2_kept", "h2_in", "adjt_in", "out_stored"))
    x_bt, y_act, y_leaky, o_mm, x1_ready, dve_a, cen_ready, sq_ready, var2_ready, rstd2_ready, h2_ready, \
        h2_turned, h2t_ready = (sem(n) for n in (
            "x_bt", "y_act", "y_leaky", "o_mm", "x1_ready", "dve_a", "cen_ready", "sq_ready", "var2_ready",
            "rstd2_ready", "h2_ready", "h2_turned", "h2t_ready"))
    mask_set, den_mm, den_low, hw_mm, dve_b, shifted, expd, hwn_ready, att_mm, neg_ready, neg_exp, elu_ready, \
        out_ready = (sem(n) for n in (
            "mask_set", "den_mm", "den_low", "hw_mm", "dve_b", "shifted", "expd", "hwn_ready", "att_mm",
            "neg_ready", "neg_exp", "elu_ready", "out_ready"))

    def at(i, q):
        return i * NS + q + 1

    def bc(v, n=128):
        return v.unsqueeze(2).broadcast_to([v.shape[0], v.shape[1], n])

    def graphs(i, q):
        return bass.ds((i * NS + q) * 4, 4)

    def flat(t):
        return t.rearrange("p b n -> p (b n)")

    def loop(eng, body):
        body(0, True)
        with eng.Fori(1, NI) as i:
            body(i, False)

    def sync(sp, x_n, out_n, adj_tn, h_nat, h_tr, y_ready):
        sp.wait_ge(y_ready, NQ)

        def loads_a(i, first):
            for q in range(NS):
                if not first:
                    sp.wait_ge(x1_ready, at(i - 1, q))
                    sp.wait_ge(o_mm, at(i - 1, q))
                sp.dma_start(X[q], x_n[:, graphs(i, q), :]).then_inc(x_in2[q], 16)
                sp.dma_start(H[q], h_tr[:, graphs(i, q), :]).then_inc(h_in2[q], 16)

        def stores_a(i):
            for q in range(NS):
                sp.wait_ge(x1_ready, at(i, q))
                sp.dma_start(h_nat[:, graphs(i, q), :], X1[q]).then_inc(x1_kept[q], 16)

        loads_a(0, True)
        with sp.Fori(1, NI) as i:
            loads_a(i, False)
            stores_a(i - 1)
        stores_a(NI - 1)
        for q in range(NS):
            sp.wait_ge(x1_kept[q], NI * 16)
            sp.wait_ge(h2_kept[q], NI * 16)

        def loads_b(i, first):
            for q in range(NS):
                if not first:
                    sp.wait_ge(att_mm, at(i - 1, q))
                    sp.wait_ge(mask_set, at(i - 1, q))
                sp.dma_start(H2T[q], h_tr[:, graphs(i, q), :]).then_inc(h2_in[q], 16)
                sp.dma_start(adjt[q], adj_tn[:, graphs(i, q), :]).then_inc(adjt_in[q], 16)

        def stores(i):
            for q in range(NS):
                sp.wait_ge(out_ready, at(i, q))
                sp.dma_start(out_n[:, graphs(i, q), :], OUT[q]).then_inc(out_stored[q], 16)

        loads_b(0, True)
        with sp.Fori(1, NI) as i:
            loads_b(i, False)
            stores(i - 1)
        stores(NI - 1)
        for q in range(NS):
            sp.wait_ge(out_stored[q], 16 * NI)

    def gpsimd(pool, bt_sb, minus_half):
        def body_a(i, first):
            for q in range(NS):
                pool.wait_ge(x_in2[q], (i + 1) * 16)
                nc.gpsimd.tensor_tensor(X[q], X[q], bt_sb[:, :].unsqueeze(1).broadcast_to([128, 4, 128]),
                                        ALU.add).then_inc(x_bt, 1)
            for q in range(NS):
                pool.wait_ge(var2_ready, at(i, q))
                nc.gpsimd.tensor_tensor(small[:, q, 3, :], small[:, q, 2, :], minus_half[:, 0:4], ALU.pow)\
                  .then_inc(rstd2_ready, 1)

        loop(pool, body_a)

    def scalar(act, bag, h_nat, h_tr):
        def body_a(i, first):
            for q in range(NS):
                if not first:
                    act.wait_ge(o_mm, at(i - 1, q))
                nc.scalar.activation(Y[q], h_nat[:, graphs(i, q), :], ACT.Identity,
                                     bias=bag[:, 6:7], scale=bag[:, 4:5]).then_inc(y_act, 1)
            for q in range(NS):
                act.wait_ge(cen_ready, at(i, q))
                nc.scalar.activation(SQ[q], CEN[q], ACT.Square).then_inc(sq_ready, 1)
            for q in range(NS):
                act.wait_ge(h2_turned, at(i, q))
                if not first:
                    act.wait_ge(h2_kept[q], i * 16)
                nc.scalar.copy(HT[q], bank[q][1]).then_inc(h2t_ready, 1)
            for q in range(NS):
                act.wait_ge(h2t_ready, at(i, q))
                act.dma_start(h_tr[:, graphs(i, q), :], HT[q]).then_inc(h2_kept[q], 16)

        def body_b(i, first):
            for q in range(NS):
                act.wait_ge(den_mm, at(i, q))
                if not first:
                    act.wait_ge(att_mm, at(i - 1, q))
                nc.scalar.mul(DEN[q], bank[q][0], SLOPE1).then_inc(den_low, 1)
            for q in range(NS):
                act.wait_ge(shifted, at(i, q))
                nc.scalar.activation(DEN[q], DEN[q], ACT.Exp).then_inc(expd, 1)
            for q in range(NS):
                act.wait_ge(att_mm, at(i, q))
                if not first:
                    act.wait_ge(out_ready, at(i - 1, q))
                nc.scalar.activation(MIN[q], bank[q][1], ACT.Relu, scale=-1.0).then_inc(neg_ready, 1)
            for q in range(NS):
                act.wait_ge(neg_ready, at(i, q))
                nc.scalar.activation(MIN[q], MIN[q], ACT.Exp, scale=-1.0).then_inc(neg_exp, 1)

        loop(act, body_a)
        for q in range(NS):
            act.wait_ge(x1_kept[q], NI * 16)
            act.wait_ge(h2_kept[q], NI * 16)
        loop(act, body_b)

    def tensor(pe, wt1, wt2, l1w, w1a, w2a, ident):
        def body_a(i, first):
            for q in range(NS):
                pe.wait_ge(h_in2[q], (i + 1) * 16)
                pe.wait_ge(y_leaky, at(i, q))
                if not first:
                    pe.wait_ge(x1_ready, at(i - 1, q))
                for b in range(4):
                    nc.tensor.matmul(bank[q][0][:, b, :], H[q][:, b, :], wt1[:, :], start=True, stop=False)
                    last = nc.tensor.matmul(bank[q][0][:, b, :], Y[q][:, b, :], wt2[:, :], start=False, stop=True)
                last.then_inc(o_mm, 1)
            for q in range(NS):
                pe.wait_ge(h2_ready, at(i, q))
                if not first:
                    pe.wait_ge(h2t_ready, at(i - 1, q))
                for b in range(4):
                    last = nc.tensor.transpose(bank[q][1][:, b, :], CEN[q][:, b, :], ident[:, :])
                last.then_inc(h2_turned, 1)

        def body_b(i, first):
            for q in range(NS):
                pe.wait_ge(h2_in[q], (i + 1) * 16)
                if first:
                    pe.wait_ge(h2t_ready, NI * NS)
                else:
                    pe.wait_ge(out_ready, at(i - 1, q))
                for b in range(4):
                    nc.tensor.matmul(bank[q][0][:, b, :], w1a[:, :], H2T[q][:, b, :], start=True, stop=False)
                    last = nc.tensor.matmul(bank[q][0][:, b, :], H2T[q][:, b, :], w2a[:, :], start=False, stop=True)
                last.then_inc(den_mm, 1)
            for q in range(NS):
                for b in range(4):
                    last = nc.tensor.matmul(bank[q][1][:, b, :], H2T[q][:, b, :], l1w[:, :], start=True, stop=True)
                last.then_inc(hw_mm, 1)
            for q in range(NS):
                pe.wait_ge(hwn_ready, at(i, q))
                for b in range(4):
                    last = nc.tensor.matmul(bank[q][1][:, b, :], DEN[q][:, b, :], HWN[q][:, b, :], start=True, stop=True)
                last.then_inc(att_mm, 1)

        loop(pe, body_a)
        loop(pe, body_b)

    def vector(dve, h_nat, bn2_ready):
        LINKS_A, LINKS_B = 3, 5

        def body_a(i, first):
            steps = iter(range(1, LINKS_A * NS + 1))

            def link(ins):
                ins.then_inc(dve_a, 1)
                dve.wait_ge(dve_a, i * LINKS_A * NS + next(steps))

            for q in range(NS):
                dve.wait_ge(y_act, at(i, q))
                nc.vector.scalar_tensor_tensor(Y[q], Y[q], SLOPE0, Y[q], ALU.mult, ALU.max).then_inc(y_leaky, 1)
            for q in range(NS):
                sm = small[:, q]
                x1 = X1[q]
                if not first:
                    dve.wait_ge(x1_kept[q], i * 16)
                dve.wait_ge(o_mm, at(i, q))
                dve.wait_ge(x_bt, at(i, q))
                nc.vector.tensor_tensor(x1, bank[q][0], X[q], ALU.add).then_inc(x1_ready, 1)
                dve.wait_ge(x1_ready, at(i, q))
                link(nc.vector.tensor_reduce(sm[:, 0, :], x1, AX.X, ALU.add))
                link(nc.vector.tensor_scalar(sm[:, 0, :], sm[:, 0, :], 1.0 / C, None, ALU.mult))
                nc.vector.tensor_tensor(CEN[q], x1, bc(sm[:, 0, :]), ALU.subtract).then_inc(cen_ready, 1)
            for q in range(NS):
                sm = small[:, q]
                dve.wait_ge(sq_ready, at(i, q))
                link(nc.vector.tensor_reduce(sm[:, 1, :], SQ[q], AX.X, ALU.add))
                nc.vector.tensor_scalar(sm[:, 2, :], sm[:, 1, :], 1.0 / C, EPS, ALU.mult, ALU.add).then_inc(var2_ready, 1)
            for q in range(NS):
                dve.wait_ge(rstd2_ready, at(i, q))
                nc.vector.scalar_tensor_tensor(CEN[q], CEN[q], 0.0, bc(small[:, q, 3, :]), ALU.max, ALU.mult)\
                  .then_inc(h2_ready, 1)

        def body_b(i, first):
            steps = iter(range(1, LINKS_B * NS + 1))

            def link(ins):
                ins.then_inc(dve_b, 1)
                dve.wait_ge(dve_b, i * LINKS_B * NS + next(steps))

            for q in range(NS):
                dve.wait_ge(adjt_in[q], (i + 1) * 16)
                nc.vector.tensor_scalar(MASK[q], adjt[q], 0.0, NEG, ALU.is_le, ALU.mult).then_inc(mask_set, 1)
            for q in range(NS):
                sm = small[:, q]
                dve.wait_ge(den_low, at(i, q))
                link(nc.vector.tensor_tensor(DEN[q], bank[q][0], DEN[q], ALU.max))
                dve.wait_ge(mask_set, at(i, q))
                link(nc.vector.tensor_tensor(DEN[q], DEN[q], MASK[q], ALU.add))
                link(nc.vector.tensor_reduce(sm[:, 0, :], DEN[q], AX.X, ALU.max))
                nc.vector.tensor_tensor(DEN[q], DEN[q], bc(sm[:, 0, :]), ALU.subtract).then_inc(shifted, 1)
            for q in range(NS):
                sm = small[:, q]
                dve.wait_ge(expd, at(i, q))
                link(nc.vector.tensor_reduce(sm[:, 1, :], DEN[q], AX.X, ALU.add))
                link(nc.vector.reciprocal(sm[:, 2, :], sm[:, 1, :]))
                dve.wait_ge(hw_mm, at(i, q))
                nc.vector.tensor_tensor(HWN[q], bank[q][1], bc(sm[:, 2, :]), ALU.mult).then_inc(hwn_ready, 1)
            for q in range(NS):
                dve.wait_ge(neg_exp, at(i, q))
                if not first:
                    dve.wait_ge(out_stored[q], i * 16)
                nc.vector.scalar_tensor_tensor(OUT[q], bank[q][1], 0.0, MIN[q], ALU.max, ALU.add).then_inc(elu_ready, 1)
            for q in range(NS):
                dve.wait_ge(elu_ready, at(i, q))
                nc.vector.scalar_tensor_tensor(OUT[q], OUT[q], -1.0, h_nat[:, graphs(i, q), :], ALU.add, ALU.add)\
                  .then_inc(out_ready, 1)

        dve.wait_ge(bn2_ready, 1)
        loop(dve, body_a)
        dve.wait_ge(h2t_ready, NI * NS)
        for q in range(NS):
            dve.wait_ge(x1_kept[q], NI * 16)
            dve.wait_ge(h2_kept[q], NI * 16)
        loop(dve, body_b)

    return dict(sync=sync, gpsimd=gpsimd, scalar=scalar, tensor=tensor, vector=vector)


def kernel(**inputs):
    import concourse.bacc as _bacc
    from concourse.bass_utils import run_bass_kernel_spmd as _run

    a = {k: np.ascontiguousarray(v) for k, v in inputs.items()}
    wt = a["L0_gnn_Wt"]
    two = lambda v: np.concatenate([v, v])
    l1a = a["L1_gnn_a"][:, 0]
    cols = np.stack([two(a["L0_gnn_g1"]), two(a["L0_gnn_be1"]), two(a["L0_gnn_b1"]), two(a["L0_gnn_W2"][0]),
                     a["L0_gnn_bg"], a["L0_gnn_gg"], a["L0_gnn_beg"], l1a[:C], l1a[C:],
                     np.broadcast_to(a["L0_gnn_b2"], (128,))], axis=1)
    node = np.arange(128)
    half = np.where(node[:, None, None] // BLK == np.arange(NBLK)[None, :, None], 0.5, 0.0)
    arrays = {
        "x": a["x"], "adj": a["adj"], "adj_t": a["adj"].transpose(0, 2, 1),
        "w1": a["L0_gnn_W1"], "w1_tt": np.concatenate([a["L0_gnn_W1"].T] * 2, axis=1),
        "wg_t": a["L0_gnn_Wg"].T, "wt1_t": wt[:, :C].T, "wt2_t": wt[:, C:].T,
        "l1_w": a["L1_gnn_W"], "l1_wt": a["L1_gnn_W"].T, "cols": cols,
        "bt_rows": np.broadcast_to(a["L0_gnn_bt"], (128, C)),
        "ident_in": np.eye(128, dtype=np.float32),
        "fold_in": (node[:, None] % MID == node[None, :] % MID).astype(np.float32),
        "half_in": np.broadcast_to(half, (128, NBLK, BLK)).astype(np.float32),
    }
    arrays = {k: np.ascontiguousarray(v) for k, v in arrays.items()}
    nc = _bacc.Bacc("TRN2", target_bir_lowering=False, num_devices=1)
    aps = [nc.dram_tensor(k, v.shape, mybir.dt.from_np(v.dtype), kind="ExternalInput").ap() for k, v in arrays.items()]
    out = nc.dram_tensor("out", (B, N, C), F32, kind="ExternalOutput").ap()
    two_layers(nc, *aps, out)
    r = _run(nc, [arrays], core_ids=[0])
    return r.results[0]["out"]
```

```python
from contextlib import ExitStack

import numpy as np

import concourse.bass as bass
from concourse import mybir

F32 = mybir.dt.float32
I32 = mybir.dt.int32
BF16 = mybir.dt.bfloat16
ALU = mybir.AluOpType
ACT = mybir.ActivationFunctionType
AX = mybir.AxisListType

B, N, C = 64, 128, 128
MID = 64
EPS = 1e-5
NEG = -9e15
SLOPE0, SLOPE1 = 0.01, 0.2
QUAD = 4
NQ = B // QUAD
PAIRS = float(B * N * N)

BLK = 8
NBLK = N // BLK
WIDE = 1024
BANK = 512
DIAG = 5
LAST = 8
CHUNKS = [[k, NBLK - 2 - k] for k in range(7)] + [[7]]
CHUNKS.insert(DIAG, None)
NCH = len(CHUNKS)
TILES = [2] * LAST + [1]
FLAT = sum(TILES) * BANK
PER = 2 * NCH
ROUNDS = 5
ROUND_END = [1, 3, 5, 7, 8]
SLOTS = 6
RECT = 2
LAG1 = 1
LAG = 3
KEEP = (0, 1, 3, 4, 6, 7)
KEPT = [k for k in range(PER) if k % NCH in KEEP]
PLAIN = [k for k in range(PER) if k % NCH not in KEEP]
NK, NP = len(KEPT), len(PLAIN)
PLAIN_SLOTS = NP // 2
ZRING = 4
TAKE = 2
COUNT = 4
LRING = 6
BY_MAX = (0, 1, 4, 6)
MAXED = [k for k in KEPT if k % NCH in BY_MAX]
COUNTED = [k for k in KEPT if k % NCH not in BY_MAX]
ABSED = [k for k in range(PER) if k not in MAXED]
NM, NC, NA = len(MAXED), len(COUNTED), len(ABSED)
PARTS = 3
NR = 2 * ROUNDS
ROUND_ENDS = [e + NCH * c for c in range(2) for e in ROUND_END]


def strip(block):
    return BLK * (block + 1), N - BLK * (block + 1)


def two_layers(nc, x, adj, adj_t, w1, w1_tt, wg_t, wt1_t, wt2_t, l1_w, l1_wt, cols, bt_rows,
               ident_in, fold_in, pair_nodes_in, half_in, out):
    flat = nc.dram_tensor("score_rows", [B, FLAT], F32, kind="Internal").ap()
    kept_dram = nc.dram_tensor("kept_products", [NQ, NK, 128, 2 * BANK], F32, kind="Internal").ap()
    x_n = x.rearrange("b n c -> n b c")
    out_n = out.rearrange("b n c -> n b c")
    adj_n = adj.rearrange("b i j -> i b j")
    adj_tn = adj_t.rearrange("b j i -> j b i")

    with ExitStack() as ctx:
        def sb(name, shape, dt=F32):
            return ctx.enter_context(nc.sbuf_tensor(name, shape, dt))

        def sem(name):
            return ctx.enter_context(nc.semaphore(name))

        w1_sb = sb("w1_sb", [MID, C])
        w1tt_sb = sb("w1tt_sb", [C, 2 * MID])
        wg_sb = sb("wg_sb", [C, C])
        wt1_sb = sb("wt1_sb", [C, C])
        wt2_sb = sb("wt2_sb", [C, C])
        l1w_sb = sb("l1w_sb", [C, C])
        l1wt_sb = sb("l1wt_sb", [C, C])
        col = sb("col", [128, 10])
        G1, BE1, B1, W2, BG, GG, BEG, A1, A2, B2 = (col[:, n:n + 1] for n in range(10))
        bt_sb = sb("bt_sb", [128, C])
        ident = sb("ident", [128, 128])
        fold = sb("fold", [128, 128])
        half = sb("half", [128, NBLK, BLK])
        minus_half = sb("minus_half", [128, 16])
        ones = sb("ones", [128, 128])
        h_nat = sb("h_nat", [N, B, C])
        h_tr = sb("h_tr", [C, B, N])
        diff = [sb(f"diff{s}", [C, 2, WIDE]) for s in range(SLOTS)]
        relu_all = sb("relu_all", [128, SLOTS, WIDE])
        relu = [relu_all[:, s, :] for s in range(SLOTS)]
        kept = [sb(f"kept{s}", [128, 2 * BANK]) for s in range(ZRING)]
        loaded = kept + [diff[SLOTS - 1][:, g, :] for g in range(2)]
        ln = sb("ln", [128, 256])
        sum_d = sb("sum_d", [128, NQ * NP])
        sum_q = sb("sum_q", [128, NQ * NP])
        kept_st = relu[0][:, 0:NQ * NC * 12].rearrange("p (n t s) -> p n t s", t=2, s=6)
        sum_p = relu[1][:, 0:NQ * NM]
        sum_m = relu[1][:, NQ * NM:2 * NQ * NM]
        w1_twice = relu[1][:, 2 * NQ * NM:2 * NQ * NM + MID]
        h_couple = [relu[2][:, 256 * c:256 * c + 256].rearrange("p (g n) -> p g n", g=2) for c in range(2)]
        y_full = relu[2][:, 512:640]
        y_rest = [relu[2][:, 640:768], relu[2][:, 768:896]]
        y_parts = [relu[3][:, 256 * c:256 * c + 64 * PARTS].bitcast(BF16)
                   .rearrange("p (s x) -> p s x", s=PARTS) for c in range(2)]
        pair_nodes = relu_all[:, 4:6, :].rearrange("p s x -> p (s x)").bitcast(BF16)
        st = sb("st", [128, 32])
        w2_rows = sb("w2_rows", [128, 32])
        lin_rows = sb("lin_rows", [C, 2, 32])
        keep_rows = sb("keep_rows", [128, 32])
        w1a = sb("w1a", [C, 128])
        w2a = sb("w2a", [C, 128])
        s_row = [sb(f"s_row{p}", [128, ROUNDS, BANK]) for p in range(2)]
        s_up = sb("s_up", [N, QUAD, N])
        s_dg = sb("s_dg", [N, QUAD, BLK])
        s_all = sb("s_all", [N, QUAD, N])
        s_shift = sb("s_shift", [N, QUAD, N])
        adj_sb = sb("adj_sb", [N, QUAD, N], I32)
        mneg = sb("mneg", [N, QUAD, N])
        prob = sb("prob", [N, QUAD, N])
        prob_tr = sb("prob_tr", [N, QUAD, N])
        h_q = sb("h_q", [N, QUAD, C])
        mix = sb("mix", [C, QUAD, N])
        rows = sb("rows", [N, 3, QUAD])
        bst = sb("bst", [C, NQ, 6])
        bag = sb("bag", [C, 8])

        psum = ctx.enter_context(nc.psum_tensor("psum", [128, 8, BANK], F32))
        prod = [psum[:, 2 * n:2 * n + 2, :] for n in range(3)]
        score = [psum[:, 6, :], psum[:, 7, :]]
        att = [psum[:, 4, :].rearrange("p (b n) -> p b n", b=QUAD),
               psum[:, 5, :].rearrange("p (b n) -> p b n", b=QUAD)]

        weights_in = sem("weights_in")
        x_in = [sem(f"x_in{g}") for g in range(4)]
        dve_ln = sem("dve_ln")
        centred = sem("centred")
        squared = sem("squared")
        var_ready = sem("var_ready")
        rstd_ready = sem("rstd_ready")
        h_ready = sem("h_ready")
        turned = sem("turned")
        h_tr_ready = sem("h_tr_ready")
        consts_set = sem("consts_set")
        wa_mm = sem("wa_mm")
        wa_ready = sem("wa_ready")

        diff_ready = [sem("diff_ready1"), sem("diff_ready2")]
        abs_ready = [sem("abs_ready1"), sem("abs_ready2")]
        prod_ready = [sem("prod_ready1"), sem("prod_ready2")]
        prod_free = sem("prod_free")
        kept_counted = sem("kept_counted")
        nodes_in = sem("nodes_in")
        nodes_ready = sem("nodes_ready")
        w1_twice_set = sem("w1_twice_set")
        couple_in = [sem("couple_in0"), sem("couple_in1")]
        w1h_mm = sem("w1h_mm")
        max_summed = sem("max_summed")
        w1h_copied = sem("w1h_copied")
        w1h_step = sem("w1h_step")
        w1h_split = sem("w1h_split")
        kept_stored = [sem(f"kept_stored{s}") for s in range(ZRING)]
        kept_in = [sem(f"kept_in{s}") for s in range(LRING)]
        lin_done = sem("lin_done")
        relu_ready = sem("relu_ready")
        shift_mm = sem("shift_mm")
        shift_ready = sem("shift_ready")
        stat = sem("stat")
        stat_sums = sem("stat_sums")
        stat_mm = sem("stat_mm")
        stat_var = sem("stat_var")
        stat_rstd = sem("stat_rstd")
        stat_lin = sem("stat_lin")
        stat_lin_mm = sem("stat_lin_mm")
        pass2_ready = sem("pass2_ready")
        round_done = sem("round_done")
        row_ready = sem("row_ready")
        rows_stored = [sem("rows_stored0"), sem("rows_stored1")]
        s_up_clear = sem("s_up_clear")
        s_in = sem("s_in")
        adj_in = sem("adj_in")
        hq_in = sem("hq_in")
        diag_set = sem("diag_set")
        s_half_ready = sem("s_half_ready")
        mask_ready = sem("mask_ready")
        s_sum = sem("s_sum")
        s_masked = sem("s_masked")
        dve_att = sem("dve_att")
        s_shifted = sem("s_shifted")
        exp_done = sem("exp_done")
        prob_ready = sem("prob_ready")
        prob_turned = sem("prob_turned")
        prob_tr_ready = sem("prob_tr_ready")
        mixed = sem("mixed")
        mix_ready = sem("mix_ready")
        y_mm = sem("y_mm")
        y_ready = sem("y_ready")
        bn2 = sem("bn2")
        bn2_var = sem("bn2_var")
        bn2_rstd = sem("bn2_rstd")
        bn2_ready = sem("bn2_ready")

        final = final_tiles(nc, sb, sem, diff, relu, psum)

        block = ctx.enter_context(nc.Block())

        def sc(n):
            return st[:, n:n + 1]

        def chunk_at(i, k):
            return i * PER + k

        def ln_sum(g):
            return ln[:, 16 * g:16 * g + 16]

        def ln_sq(g):
            return ln[:, 64 + 16 * g:80 + 16 * g]

        def ln_var(g):
            return ln[:, 128 + 16 * g:144 + 16 * g]

        def ln_rstd(g):
            return ln[:, 192 + 16 * g:208 + 16 * g]

        def group(g):
            return h_nat[:, 16 * g:16 * g + 16, :]

        def sq_tile(g):
            return diff[g][:, :, :].rearrange("p a (b c) -> p (a b) c", c=C)

        def bcast(v, n):
            return v.unsqueeze(2).broadcast_to([v.shape[0], v.shape[1], n])

        def tr_tile(g):
            return psum[:, 4 * (g % 2):4 * (g % 2) + 4, :]

        def diff_place(phase, i, k):
            if phase == 0:
                return chunk_at(i, k), k % SLOTS
            p = PLAIN.index(k)
            return i * NP + p, p % PLAIN_SLOTS

        def rounds_before(i, k):
            back = 0
            if k < 0:
                k += PER
                back = 1
            return (i - back) * NR + next(n for n, e in enumerate(ROUND_ENDS) if k <= e) + 1

        def ended(i, k, lag, depth):
            m = k - lag
            if m >= 0:
                return [(i, ROUND_ENDS.index(m))] if m in ROUND_ENDS else []
            return [(i - 1, ROUND_ENDS.index(m + PER))] if depth > 0 and m + PER in ROUND_ENDS else []

        def att_steps(table, i, k, depth):
            found = []
            if k in table and depth > 0:
                found.append((table[k], i - 1))
            if k + PER in table and depth > 1:
                found.append((table[k + PER], i - 2))
            return found

        def att_rest(table):
            return [(table[p], NQ - 2) for p in sorted(table) if p >= PER] + [(table[p], NQ - 1) for p in sorted(table)]

        @block.sync
        def _(sp):
            for g in range(4):
                sp.dma_start(h_nat[:, 16 * g:16 * g + 16, :], x_n[:, 16 * g:16 * g + 16, :]).then_inc(x_in[g], 16)
            for g in range(2):
                sp.dma_start(diff[4 + g][:, :, :].rearrange("p a x -> p (a x)"),
                             pair_nodes_in[:, 2 * WIDE * g:2 * WIDE * g + 2 * WIDE]).then_inc(nodes_in, 16)

            def store_rows(i, c):
                sp.wait_ge(row_ready, (i * 2 + c + 1) * ROUNDS)
                dst = flat[bass.ds(i * QUAD + 2 * c, 2), :]
                for q in range(4):
                    sp.dma_start(dst[:, 0:16 * BANK].rearrange("b (r q x) -> b r q x", q=4, x=BANK)[:, :, q, :],
                                 s_row[c][32 * q:32 * q + 2, 0:4, :]).then_inc(rows_stored[c], 16)
                sp.dma_start(dst[:, 16 * BANK:FLAT], s_row[c][0:2, 4, :]).then_inc(rows_stored[c], 16)

            def load_scores(i, chunks, first):
                if 0 in chunks:
                    for c in range(2):
                        sp.wait_ge(rows_stored[c], (i + 1) * 5 * 16)
                    if not first:
                        sp.wait_ge(s_half_ready, i)
                    else:
                        sp.wait_ge(s_up_clear, 1)
                src = flat[bass.ds(i * QUAD, QUAD), :]
                for k in chunks:
                    at = k * WIDE
                    if CHUNKS[k] is None:
                        sp.dma_start(s_dg[:, :, :], src[:, at:at + WIDE].rearrange("b (p j) -> p b j", j=BLK))\
                          .then_inc(s_in, 16)
                        continue
                    for blk in CHUNKS[k]:
                        j0, n = strip(blk)
                        sp.dma_start(s_up[BLK * blk:BLK * blk + BLK, :, j0:N],
                                     src[:, at:at + BLK * n].rearrange("b (p j) -> p b j", j=n))\
                          .then_inc(s_in, 16)
                        at += BLK * n

            def load_adj(i, first):
                if not first:
                    sp.wait_ge(mask_ready, i)
                sp.dma_start(adj_sb[:, :, :], adj_n[:, bass.ds(i * QUAD, QUAD), :]).then_inc(adj_in, 16)

            def load_h(i, first):
                if not first:
                    sp.wait_ge(mixed, i)
                sp.dma_start(h_q[:, :, :], h_nat[:, bass.ds(i * QUAD, QUAD), :]).then_inc(hq_in, 16)

            def load_couple(i, c):
                if not isinstance(i, int) or i > 0:
                    sp.wait_ge(w1h_mm, 2 * i + c - 1)
                sp.dma_start(h_couple[c], h_tr[:, bass.ds(i * QUAD + 2 * c, 2), :]).then_inc(couple_in[c], 16)

            def store_kept(i, last):
                for n in range(NK):
                    if n == 0:
                        load_couple(i, 1)
                    if n == 6 and not last:
                        load_couple(i + 1, 0)
                    sp.wait_ge(prod_free, chunk_at(i, KEPT[n]) + 1)
                    sp.dma_start(kept_dram[bass.ds(i, 1), n, :, :].rearrange("a p x -> p (a x)"),
                                 kept[n % ZRING][:, :]).then_inc(kept_stored[n % ZRING], 16)

            sp.wait_ge(h_tr_ready, 4)
            load_couple(0, 0)
            store_kept(0, False)
            with sp.Fori(1, NQ - 1) as i:
                store_kept(i, False)
            store_kept(NQ - 1, True)
            for z in range(ZRING):
                sp.wait_ge(kept_stored[z], NQ * NK // ZRING * 16)
            sp.wait_ge(kept_counted, NQ * NC)
            sp.wait_ge(prod_ready[0], NQ * PER)

            def load_kept(i, n, depth):
                if depth > 0 or n >= LRING:
                    back, m = (0, n - LRING) if n >= LRING else (1, n - LRING + NK)
                    sp.wait_ge(round_done, rounds_before(i - back, KEPT[m]))
                sp.dma_start(loaded[n % LRING][:, :],
                             kept_dram[bass.ds(i, 1), n, :, :].rearrange("a p x -> p (a x)"))\
                  .then_inc(kept_in[n % LRING], 16)

            def graphs(i, depth):
                for n in range(NK):
                    if n == 2 and depth > 0:
                        store_rows(i - 1, 0)
                    if n == 6 and depth > 0:
                        store_rows(i - 1, 1)
                        load_adj(i - 1, depth == 1)
                    if n > 6 and depth > 0:
                        load_scores(i - 1, range(2 * (n - 7), min(2 * (n - 6), NCH)), depth == 1)
                    load_kept(i, n, depth)
                if depth > 0:
                    load_h(i - 1, depth == 1)

            graphs(0, 0)
            graphs(1, 1)
            with sp.Fori(2, NQ) as i:
                graphs(i, 2)
            store_rows(NQ - 1, 0)
            store_rows(NQ - 1, 1)
            load_adj(NQ - 1, False)
            load_scores(NQ - 1, range(NCH), False)
            load_h(NQ - 1, False)
            final["sync"](sp, x_n, out_n, adj_tn, h_nat, h_tr, y_ready)

        @block.gpsimd
        def _(pool):
            nc.gpsimd.memset(minus_half[:, :], -0.5)
            nc.gpsimd.memset(ones[:, :], 1.0)
            nc.gpsimd.memset(w2_rows[:, :], 0.0)
            nc.gpsimd.memset(keep_rows[:, :], 0.0)
            nc.gpsimd.memset(lin_rows[:, :, :], 0.0).then_inc(consts_set, 1)
            nc.gpsimd.memset(s_up[:, :, :], 0.0).then_inc(s_up_clear, 1)
            pool.wait_ge(consts_set, 1)
            for g in range(4):
                pool.wait_ge(var_ready, g + 1)
                nc.gpsimd.tensor_tensor(ln_rstd(g), ln_var(g), minus_half[:, 0:16], ALU.pow).then_inc(rstd_ready, 1)
            pool.wait_ge(nodes_in, 32)
            for g in range(2):
                nc.gpsimd.tensor_copy(pair_nodes[:, 2 * WIDE * g:2 * WIDE * g + 2 * WIDE],
                                      diff[4 + g][:, :, :].rearrange("p a x -> p (a x)")).then_inc(nodes_ready, 1)

            def split(i, c):
                full = [y_full, y_rest[0], y_rest[1]]
                if not isinstance(i, int) or i > 0:
                    pool.wait_ge(prod_ready[0], chunk_at(i - 1, NCH * c + BY_MAX[-1]) + 1)
                pool.wait_ge(w1h_copied, 2 * i + c + 1)
                for n in range(PARTS):
                    nc.gpsimd.tensor_tensor(y_parts[c][:, n, :], full[n], ones[:, :], ALU.mult)\
                      .then_inc(w1h_step if n < PARTS - 1 else w1h_split, 1)
                    if n < PARTS - 1:
                        pool.wait_ge(w1h_step, (2 * i + c) * 4 + 2 * n + 1)
                        nc.gpsimd.tensor_tensor(full[n + 1], full[n], y_parts[c][:, n, :], ALU.subtract)\
                          .then_inc(w1h_step, 1)
                        pool.wait_ge(w1h_step, (2 * i + c) * 4 + 2 * n + 2)

            split(0, 0)
            split(0, 1)
            with pool.Fori(1, NQ) as i:
                split(i, 0)
                split(i, 1)
            pool.wait_ge(stat_var, 1)
            nc.gpsimd.tensor_tensor(sc(11), sc(10), minus_half[:, 0:1], ALU.pow).then_inc(stat_rstd, 1)

            def assemble(i):
                pool.wait_ge(s_in, (i + 1) * 16 * 16)
                if not isinstance(i, int) or i > 0:
                    pool.wait_ge(s_sum, i)
                nc.gpsimd.tensor_tensor(s_all[:, :, :].rearrange("p b (k j) -> p b k j", j=BLK),
                                        s_dg[:, :, :].unsqueeze(2).broadcast_to([N, QUAD, NBLK, BLK]),
                                        half[:, :, :].unsqueeze(1).broadcast_to([N, QUAD, NBLK, BLK]),
                                        ALU.mult).then_inc(diag_set, 1)
                pool.wait_ge(adj_in, (i + 1) * 16)
                if not isinstance(i, int) or i > 0:
                    pool.wait_ge(s_masked, i)
                pool.wait_ge(diag_set, i + 1)
                nc.gpsimd.tensor_tensor(s_all[:, :, :], s_all[:, :, :], s_up[:, :, :], ALU.add)\
                  .then_inc(s_half_ready, 1)
                nc.gpsimd.tensor_scalar(mneg[:, :, :], adj_sb[:, :, :], 0.0, NEG, ALU.is_le, ALU.mult)\
                  .then_inc(mask_ready, 1)

            pool.wait_ge(weights_in, 16 * 12)
            assemble(0)
            with pool.Fori(1, NQ) as i:
                assemble(i)
            pool.wait_ge(bn2_var, 1)
            nc.gpsimd.tensor_tensor(bag[:, 3:4], bag[:, 2:3], minus_half[:, 0:1], ALU.pow).then_inc(bn2_rstd, 1)
            final["gpsimd"](pool, bt_sb, minus_half)

        @block.scalar
        def _(act):
            for t, src in ((w1_sb, w1), (w1tt_sb, w1_tt), (wg_sb, wg_t), (wt1_sb, wt1_t), (wt2_sb, wt2_t),
                           (l1w_sb, l1_w), (l1wt_sb, l1_wt), (col, cols), (bt_sb, bt_rows),
                           (ident, ident_in), (fold, fold_in)):
                act.dma_start(t[:, :], src).then_inc(weights_in, 16)
            act.dma_start(half[:, :, :], half_in).then_inc(weights_in, 16)
            for g in range(4):
                act.wait_ge(centred, g + 1)
                nc.scalar.activation(sq_tile(g), group(g), ACT.Square).then_inc(squared, 1)
                if g > 0:
                    act.wait_ge(turned, g)
                    nc.scalar.copy(h_tr[:, 16 * g - 16:16 * g, :], tr_tile(g - 1)).then_inc(h_tr_ready, 1)
            act.wait_ge(turned, 4)
            nc.scalar.copy(h_tr[:, 48:64, :], tr_tile(3)).then_inc(h_tr_ready, 1)

            def absolute(phase, i, k):
                n = WIDE if k % NCH != LAST else BANK
                at, slot = diff_place(phase, i, k)
                if phase == 0 and k in MAXED:
                    return
                act.wait_ge(diff_ready[phase], at + 1)
                tile = diff[slot][:, :, 0:n]
                acc = sum_d[:, bass.ds(i * NP + PLAIN.index(k), 1)] if phase == 0 and k in PLAIN else None
                nc.scalar.activation(tile, tile, ACT.Abs, accum_out=acc).then_inc(abs_ready[phase], 1)

            def take(i, k, depth, shift_wait=False):
                t = TILES[k % NCH]
                act.wait_ge(prod_ready[0], chunk_at(i, k) + 1)
                tile = prod[k % 3][:, 0:t, :]
                if k in PLAIN:
                    nc.scalar.activation(tile, tile, ACT.Square, bias=sc(0),
                                         accum_out=sum_q[:, bass.ds(i * NP + PLAIN.index(k), 1)]).then_inc(prod_free, 1)
                    return
                n = KEPT.index(k)
                if depth > 0 or n >= ZRING:
                    back, m = (0, n - ZRING) if n >= ZRING else (1, n - ZRING + NK)
                    if KEPT[m] in COUNTED:
                        act.wait_ge(kept_counted, (i - back) * NC + COUNTED.index(KEPT[m]) + 1)
                    act.wait_ge(kept_stored[n % ZRING], (i * (NK // ZRING) + n // ZRING) * 16)
                if k in COUNTED:
                    nc.scalar.copy(kept[n % ZRING][:, :], tile.rearrange("p a b -> p (a b)")).then_inc(prod_free, 1)
                    return
                m = MAXED.index(k)
                nc.scalar.activation(kept[n % ZRING][:, :], tile.rearrange("p a b -> p (a b)"), ACT.Identity,
                                     accum_out=sum_p[:, bass.ds(i * NM + m, 1)]).then_inc(max_summed, 1)
                if shift_wait:
                    act.wait_ge(shift_ready, 1)
                nc.scalar.activation(tile, tile, ACT.Square, bias=sc(0),
                                     accum_out=sum_m[:, bass.ds(i * NM + m, 1)]).then_inc(prod_free, 1)

            def copy_w1h(i, c):
                act.wait_ge(w1h_mm, 2 * i + c + 1)
                if not isinstance(i, int) or i > 0 or c > 0:
                    act.wait_ge(w1h_split, 2 * i + c)
                nc.scalar.copy(y_full, score[1][:, 0:128]).then_inc(w1h_copied, 1)

            def pass1_body(i, first, last=False):
                for k in range(PER):
                    absolute(0, i, k)
                    if k >= TAKE:
                        take(i, k - TAKE, 0 if first else 1, first and k == TAKE)
                    elif not first:
                        take(i - 1, k - TAKE + PER, 1)
                    if k == 5:
                        copy_w1h(i, 1)
                    if k == 13 and not last:
                        copy_w1h(i + 1, 0)

            copy_w1h(0, 0)
            pass1_body(0, True)
            with act.Fori(1, NQ - 1) as i:
                pass1_body(i, False)
            pass1_body(NQ - 1, False, True)
            for k in range(PER - TAKE, PER):
                take(NQ - 1, k, 1)

            def rectify(i, k, depth):
                t = TILES[k % NCH]
                if depth > 0 or k >= SLOTS:
                    act.wait_ge(round_done, rounds_before(i, k - SLOTS))
                if k in PLAIN:
                    p = PLAIN.index(k)
                    act.wait_ge(prod_ready[1], i * NP + p + 1)
                    src = prod[p % 2][:, 0:t, :].rearrange("p a b -> p (a b)")
                else:
                    n = KEPT.index(k)
                    act.wait_ge(kept_in[n % LRING], (i * (NK // LRING) + n // LRING + 1) * 16)
                    src = loaded[n % LRING][:, :]
                nc.scalar.activation(relu[k % SLOTS][:, 0:t * BANK], src, ACT.Relu, bias=sc(14), scale=sc(12))\
                  .then_inc(relu_ready, 1)

            def exps(i):
                act.wait_ge(s_shifted, i + 1)
                nc.scalar.activation(prob[:, :, :], s_shift[:, :, :], ACT.Exp).then_inc(exp_done, 1)

            def pass2_body(i, depth):
                for k in range(PER):
                    if k in PLAIN:
                        absolute(1, i, k)
                    if k >= RECT:
                        rectify(i, k - RECT, depth)
                    elif depth > 0:
                        rectify(i - 1, k - RECT + PER, depth - 1)
                    for step, j in att_steps({25: exps}, i, k, depth):
                        step(j)

            act.wait_ge(pass2_ready, 1)
            pass2_body(0, 0)
            pass2_body(1, 1)
            with act.Fori(2, NQ) as i:
                pass2_body(i, 2)
            for k in range(PER - RECT, PER):
                rectify(NQ - 1, k, 2)
            exps(NQ - 2)
            exps(NQ - 1)
            act.wait_ge(bn2_ready, 1)
            final["scalar"](act, bag, h_nat, h_tr)

        @block.tensor
        def _(pe):
            pe.wait_ge(weights_in, 16 * 12)
            nc.tensor.matmul(psum[:, 0, 0:1], l1wt_sb[:, :], A1, start=True, stop=True)
            nc.tensor.matmul(psum[:, 0, 1:2], l1wt_sb[:, :], A2, start=True, stop=True).then_inc(wa_mm, 1)
            pe.wait_ge(wa_ready, 1)
            for g in range(4):
                pe.wait_ge(h_ready, g + 1)
                if g >= 2:
                    pe.wait_ge(h_tr_ready, g - 1)
                for b in range(16):
                    last = nc.tensor.transpose(tr_tile(g)[:, b // 4, 128 * (b % 4):128 * (b % 4) + 128],
                                               h_nat[:, 16 * g + b, :], ident[:, :])
                last.then_inc(turned, 1)
            pe.wait_ge(h_tr_ready, 4)

            def products(phase, i, k):
                at, slot = diff_place(phase, i, k)
                n = k % 3 if phase == 0 else PLAIN.index(k) % 2
                pe.wait_ge(abs_ready[phase], i * NA + ABSED.index(k) + 1 if phase == 0 else at + 1)
                for t in range(TILES[k % NCH]):
                    for g in range(2):
                        last = nc.tensor.matmul(prod[n][MID * g:MID * g + MID, t, :], w1tt_sb[:, 0:MID],
                                                diff[slot][:, g, t * BANK:t * BANK + BANK],
                                                start=True, stop=True)
                last.then_inc(prod_ready[phase], 1)

            def products_by_max(i, k):
                at, slot = diff_place(0, i, k)
                c = k // NCH
                m = BY_MAX.index(k % NCH)
                pe.wait_ge(w1h_split, 2 * i + c + 1)
                pe.wait_ge(diff_ready[0], at + 1)
                for t in range(2):
                    for g in range(2):
                        nc.tensor.matmul(prod[k % 3][MID * g:MID * g + MID, t, :], w1_twice,
                                         diff[slot][:, g, t * BANK:t * BANK + BANK], start=True, stop=False)
                    for n in range(PARTS):
                        for g in range(2):
                            last = nc.tensor.matmul(prod[k % 3][MID * g:MID * g + MID, t, :],
                                                    y_parts[c][:, n, MID * g:MID * g + MID],
                                                    pair_nodes[:, m * WIDE + t * BANK:m * WIDE + t * BANK + BANK],
                                                    start=False, stop=(n == PARTS - 1))
                last.then_inc(prod_ready[0], 1)

            def w1h(i, c):
                pe.wait_ge(couple_in[c], (i + 1) * 16)
                if not isinstance(i, int) or i > 0 or c > 0:
                    pe.wait_ge(w1h_copied, 2 * i + c)
                for g in range(2):
                    last = nc.tensor.matmul(score[1][:, MID * g:MID * g + MID], h_couple[c][:, g, :],
                                            w1tt_sb[:, 0:MID], start=True, stop=True)
                last.then_inc(w1h_mm, 1)

            def pass1_body(i, first, final_one=False):
                for k in range(PER):
                    if not (first and k < 3):
                        pe.wait_ge(prod_free, chunk_at(i, k) - 2)
                    if k in MAXED:
                        products_by_max(i, k)
                    else:
                        products(0, i, k)
                    if k == 3:
                        w1h(i, 1)
                    if k == 11 and not final_one:
                        w1h(i + 1, 0)
                    if first and k == 1:
                        pe.wait_ge(max_summed, 1)
                        nc.tensor.matmul(score[0][:, 0:1], fold[:, :], sum_p[:, 0:1],
                                         start=True, stop=True).then_inc(shift_mm, 1)

            w1h(0, 0)
            pe.wait_ge(w1_twice_set, 1)
            pe.wait_ge(nodes_ready, 2)
            pass1_body(0, True)
            with pe.Fori(1, NQ - 1) as i:
                pass1_body(i, False)
            pass1_body(NQ - 1, False, True)

            pe.wait_ge(stat_sums, 1)
            nc.tensor.matmul(score[0][:, 1:2], w1tt_sb[:, :], sc(3), start=True, stop=False)
            nc.tensor.matmul(score[0][:, 1:2], fold[:, :], sc(22), start=False, stop=True)
            nc.tensor.matmul(score[0][:, 2:3], fold[:, :], sc(6), start=True, stop=True).then_inc(stat_mm, 1)
            pe.wait_ge(stat_lin, 1)
            nc.tensor.matmul(score[0][:, 3:4], w1_sb[:, :], st[0:MID, 16:17], start=True, stop=True)
            nc.tensor.matmul(score[0][:, 4:5], ones[0:MID, :], st[0:MID, 17:18], start=True, stop=True).then_inc(stat_lin_mm, 1)
            pe.wait_ge(pass2_ready, 1)

            def parts(done):
                c, r = divmod(done, ROUNDS)
                return [(q, c * NCH + (4 * r + q) // 2, q % 2) for q in range(4 if r < ROUNDS - 1 else 1)]

            def slopes(i, done, depth):
                if depth > 0 or done >= 2:
                    pe.wait_ge(row_ready, i * NR + done - 1)
                bank = score[done % 2]
                tiles = parts(done)
                for g in range(2):
                    for q, k, t in tiles:
                        if k in PLAIN:
                            slot = diff_place(1, 0, k)[1]
                            last = nc.tensor.matmul(bank[32 * q:32 * q + 32, :], lin_rows[:, g, :],
                                                    diff[slot][:, g, t * BANK:t * BANK + BANK],
                                                    start=(g == 0), stop=False)
                        elif g == 0:
                            n = KEPT.index(k)
                            if t == 0:
                                pe.wait_ge(kept_in[n % LRING], (i * (NK // LRING) + n // LRING + 1) * 16)
                            last = nc.tensor.matmul(bank[32 * q:32 * q + 32, :], keep_rows[:, :],
                                                    loaded[n % LRING][:, t * BANK:t * BANK + BANK],
                                                    start=True, stop=False)
                last.then_inc(lin_done, 1)

            def scores(i, done):
                pe.wait_ge(relu_ready, chunk_at(i, ROUND_ENDS[done]) + 1)
                for q, k, t in parts(done):
                    last = nc.tensor.matmul(score[done % 2][32 * q:32 * q + 32, :], w2_rows[:, :],
                                            relu[k % SLOTS][:, t * BANK:t * BANK + BANK], start=False, stop=True)
                last.then_inc(round_done, 1)

            def att_sum(i):
                pe.wait_ge(s_half_ready, i + 1)
                for b in range(QUAD):
                    nc.tensor.matmul(att[0][:, b, :], ident[:, :], s_all[:, b, :], start=True, stop=False)
                    last = nc.tensor.matmul(att[0][:, b, :], s_all[:, b, :], ident[:, :], start=False, stop=True)
                last.then_inc(s_sum, 1)

            def att_turn(i):
                pe.wait_ge(prob_ready, i + 1)
                for b in range(QUAD):
                    last = nc.tensor.transpose(att[1][:, b, :], prob[:, b, :], ident[:, :])
                last.then_inc(prob_turned, 1)

            def att_mix(i):
                pe.wait_ge(prob_tr_ready, i + 1)
                pe.wait_ge(hq_in, (i + 1) * 16)
                for b in range(QUAD):
                    last = nc.tensor.matmul(att[0][:, b, :], h_q[:, b, :], prob_tr[:, b, :], start=True, stop=True)
                last.then_inc(mixed, 1)

            def att_out(i):
                pe.wait_ge(mix_ready, i + 1)
                nc.tensor.matmul(psum[:, 5, :], wg_sb[:, :], mix[:, :, :].rearrange("p b n -> p (b n)"),
                                 start=True, stop=True).then_inc(y_mm, 1)

            ATT = {22: att_sum, 27: att_turn, 29: att_mix, 31: att_out}

            def pass2_body(i, depth):
                for k in range(PER):
                    if k in PLAIN:
                        p = PLAIN.index(k)
                        if depth > 0 or p >= 2:
                            back, m = (0, p - 2) if p >= 2 else (1, p - 2 + NP)
                            pe.wait_ge(relu_ready, chunk_at(i - back, PLAIN[m]) + 1)
                        products(1, i, k)
                    for j, done in ended(i, k, LAG, depth):
                        scores(j, done)
                    for j, done in ended(i, k, LAG1, depth):
                        slopes(j, done, depth)
                    for step, j in att_steps(ATT, i, k, depth):
                        step(j)

            pass2_body(0, 0)
            pass2_body(1, 1)
            with pe.Fori(2, NQ) as i:
                pass2_body(i, 2)
            for k in range(LAG):
                for j, done in ended(NQ, k, LAG, 2):
                    scores(j, done)
                if k < LAG1:
                    for j, done in ended(NQ, k, LAG1, 2):
                        slopes(j, done, 2)
            for step, j in att_rest(ATT):
                step(j)
            final["tensor"](pe, wt1_sb, wt2_sb, l1w_sb, w1a, w2a, ident)

        @block.vector
        def _(dve):
            count = [0]

            def ln_step(ins):
                count[0] += 1
                ins.then_inc(dve_ln, 1)
                return count[0]

            def centre(g):
                dve.wait_ge(x_in[g], 16)
                dve.wait_ge(dve_ln, ln_step(nc.vector.tensor_reduce(ln_sum(g), group(g), AX.X, ALU.add)))
                dve.wait_ge(dve_ln, ln_step(nc.vector.tensor_scalar(ln_sum(g), ln_sum(g), 1.0 / C, None, ALU.mult)))
                nc.vector.tensor_tensor(group(g), group(g), bcast(ln_sum(g), C), ALU.subtract).then_inc(centred, 1)

            def scale(g):
                dve.wait_ge(squared, g + 1)
                dve.wait_ge(dve_ln, ln_step(nc.vector.tensor_reduce(ln_sq(g), sq_tile(g), AX.X, ALU.add)))
                nc.vector.tensor_scalar(ln_var(g), ln_sq(g), 1.0 / C, EPS, ALU.mult, ALU.add).then_inc(var_ready, 1)
                dve.wait_ge(rstd_ready, g + 1)
                nc.vector.scalar_tensor_tensor(group(g), group(g), 0.0, bcast(ln_rstd(g), C), ALU.max, ALU.mult)\
                  .then_inc(h_ready, 1)

            dve.wait_ge(wa_mm, 1)
            dve.wait_ge(weights_in, 16 * 12)
            nc.vector.tensor_scalar(w1_twice, w1tt_sb[:, 0:MID], 2.0, None, ALU.mult).then_inc(w1_twice_set, 1)
            nc.vector.tensor_copy(w1a[:, :], psum[:, 0, 0:1].broadcast_to([C, 128]))
            nc.vector.tensor_copy(w2a[:, :], psum[:, 0, 1:2].broadcast_to([C, 128])).then_inc(wa_ready, 1)
            centre(0)
            for g in range(4):
                if g < 3:
                    centre(g + 1)
                scale(g)
            dve.wait_ge(h_tr_ready, 4)

            def differences(phase, i, k, depth):
                at, slot = diff_place(phase, i, k)
                if phase == 0 and (depth > 0 or k >= SLOTS):
                    dve.wait_ge(prod_ready[0], at - SLOTS + 1)
                elif phase == 1 and (depth > 0 or k >= NCH):
                    dve.wait_ge(lin_done, rounds_before(i, k - NCH))
                c, m = divmod(k, NCH)
                tile = diff[slot]
                two = h_tr[:, bass.ds(i * QUAD + 2 * c, 2), :]
                op = ALU.max if phase == 0 and k in MAXED else ALU.subtract
                if CHUNKS[m] is None:
                    for g in range(2):
                        one = h_tr[:, bass.ds(i * QUAD + 2 * c + g, 1), :].rearrange("p a (k j) -> p (a k) j", j=BLK)
                        last = nc.vector.tensor_tensor(
                            tile[:, g, :].rearrange("p (k i j) -> p k i j", i=BLK, j=BLK),
                            one.unsqueeze(2).broadcast_to([C, NBLK, BLK, BLK]),
                            one.unsqueeze(3).broadcast_to([C, NBLK, BLK, BLK]), ALU.subtract)
                    last.then_inc(diff_ready[phase], 1)
                    return
                at = 0
                for blk in CHUNKS[m]:
                    j0, n = strip(blk)
                    last = nc.vector.tensor_tensor(
                        tile[:, :, at:at + BLK * n].rearrange("p a (i j) -> p a i j", j=n),
                        two[:, :, j0:N].unsqueeze(2).broadcast_to([C, 2, BLK, n]),
                        two[:, :, j0 - BLK:j0].unsqueeze(3).broadcast_to([C, 2, BLK, n]), op)
                    at += BLK * n
                last.then_inc(diff_ready[phase], 1)

            def count_kept(i, k):
                n = KEPT.index(k)
                dve.wait_ge(prod_free, chunk_at(i, k) + 1)
                for t in range(2):
                    last = nc.vector.bn_stats(kept_st[:, bass.ds(i * NC + COUNTED.index(k), 1), t, :].rearrange("p a s -> p (a s)"),
                                              kept[n % ZRING][:, t * BANK:t * BANK + BANK])
                last.then_inc(kept_counted, 1)

            def pass1_body(i, first):
                for k in range(PER):
                    differences(0, i, k, 0 if first else 1)
                    if k - COUNT in COUNTED:
                        count_kept(i, k - COUNT)
                    elif k - COUNT + PER in COUNTED and not first:
                        count_kept(i - 1, k - COUNT + PER)
                    if first and k == TAKE + 1:
                        dve.wait_ge(shift_mm, 1)
                        nc.vector.tensor_scalar(sc(0), score[0][:, 0:1], -0.5 / WIDE, None, ALU.mult)\
                          .then_inc(shift_ready, 1)

            dve.wait_ge(nodes_ready, 2)
            pass1_body(0, True)
            with dve.Fori(1, NQ) as i:
                pass1_body(i, False)
            for k in range(PER - COUNT, PER):
                if k in COUNTED:
                    count_kept(NQ - 1, k)

            done = [0]

            def then(ins):
                done[0] += 1
                ins.then_inc(stat, 1)
                dve.wait_ge(stat, done[0])

            dve.wait_ge(prod_free, NQ * PER)
            dve.wait_ge(kept_counted, NQ * NC)
            v_d = sum_d[:, :].rearrange("p (q k) -> p q k", k=NP // 2)[:, :, PLAIN.index(DIAG)]
            v_q = sum_q[:, :].rearrange("p (q k) -> p q k", k=NP // 2)[:, :, PLAIN.index(DIAG)]
            nc.vector.tensor_reduce(sc(1), sum_d[:, :], AX.X, ALU.add)
            nc.vector.tensor_reduce(sc(2), v_d, AX.X, ALU.add)
            nc.vector.tensor_reduce(sc(24), sum_p, AX.X, ALU.add)
            nc.vector.tensor_reduce(sc(25), sum_m, AX.X, ALU.add)
            nc.vector.tensor_reduce(sc(4), sum_q[:, :], AX.X, ALU.add)
            then(nc.vector.tensor_reduce(sc(5), v_q, AX.X, ALU.add))
            nc.vector.scalar_tensor_tensor(sc(3), sc(1), 2.0, sc(2), ALU.mult, ALU.subtract)
            then(nc.vector.scalar_tensor_tensor(sc(6), sc(4), 2.0, sc(5), ALU.mult, ALU.subtract))
            kept_n = float(2 * NQ * NC * 2 * BANK)
            then(nc.vector.scalar_tensor_tensor(sc(6), sc(25), 2.0, sc(6), ALU.mult, ALU.add))
            then(nc.vector.bn_aggr(st[:, 20:22], kept_st[:, :, :, :].rearrange("p n t s -> p (n t s)")))
            then(nc.vector.tensor_scalar(sc(22), sc(20), kept_n, None, ALU.mult))
            nc.vector.scalar_tensor_tensor(sc(22), sc(24), 2.0, sc(22), ALU.mult, ALU.add)
            then(nc.vector.tensor_tensor(sc(23), sc(20), sc(0), ALU.add))
            then(nc.vector.tensor_tensor(sc(23), sc(23), sc(23), ALU.mult))
            then(nc.vector.tensor_tensor(sc(23), sc(23), sc(21), ALU.add))
            nc.vector.scalar_tensor_tensor(sc(6), sc(23), kept_n, sc(6), ALU.mult, ALU.add).then_inc(stat_sums, 1)
            dve.wait_ge(stat_mm, 1)
            then(nc.vector.tensor_scalar(sc(7), score[0][:, 1:2], 1.0 / PAIRS, None, ALU.mult))
            then(nc.vector.tensor_tensor(sc(8), sc(7), sc(0), ALU.add))
            then(nc.vector.tensor_tensor(sc(9), sc(8), sc(8), ALU.mult))
            then(nc.vector.scalar_tensor_tensor(sc(9), score[0][:, 2:3], 1.0 / PAIRS, sc(9), ALU.mult, ALU.subtract))
            nc.vector.tensor_scalar(sc(10), sc(9), EPS, None, ALU.add).then_inc(stat_var, 1)
            dve.wait_ge(stat_rstd, 1)
            then(nc.vector.tensor_tensor(sc(12), sc(11), G1, ALU.mult))
            then(nc.vector.tensor_tensor(sc(13), sc(7), B1, ALU.add))
            then(nc.vector.tensor_tensor(sc(13), B1, sc(13), ALU.subtract))
            then(nc.vector.tensor_tensor(sc(14), sc(13), sc(12), ALU.mult))
            then(nc.vector.tensor_tensor(sc(14), sc(14), BE1, ALU.add))
            then(nc.vector.tensor_scalar(sc(15), W2, SLOPE0, None, ALU.mult))
            then(nc.vector.tensor_tensor(sc(16), sc(15), sc(12), ALU.mult))
            nc.vector.tensor_tensor(sc(17), sc(15), sc(14), ALU.mult).then_inc(stat_lin, 1)
            for g in range(2):
                part = slice(MID * g, MID * g + MID)
                nc.vector.tensor_scalar(w2_rows[part, g:g + 1], col[part, 3:4], 1.0 - SLOPE0, None, ALU.mult)
                nc.vector.tensor_copy(keep_rows[part, g:g + 1], st[part, 16:17])
            dve.wait_ge(stat_lin_mm, 1)
            for g in range(2):
                nc.vector.tensor_copy(lin_rows[:, g, g:g + 1], score[0][:, 3:4])
            nc.vector.tensor_tensor(sc(18), score[0][:, 4:5], B2, ALU.add).then_inc(pass2_ready, 1)
            dve.wait_ge(pass2_ready, 1)

            def evacuate(i, done, depth):
                c, r = divmod(done, ROUNDS)
                dve.wait_ge(round_done, i * NR + done + 1)
                if depth > 0:
                    dve.wait_ge(rows_stored[c], i * 80)
                p = 128 if r < ROUNDS - 1 else 32
                nc.vector.tensor_copy(s_row[c][0:p, r, :], score[done % 2][0:p, :]).then_inc(row_ready, 1)

            def link(i, n, ins):
                ins.then_inc(dve_att, 1)
                dve.wait_ge(dve_att, i * 4 + n)

            def att_scores(i):
                dve.wait_ge(s_sum, i + 1)
                dve.wait_ge(mask_ready, i + 1)
                nc.vector.scalar_tensor_tensor(s_shift[:, :, :], att[0], sc(18), mneg[:, :, :], ALU.add, ALU.add)\
                  .then_inc(s_masked, 1)
                dve.wait_ge(s_masked, i + 1)
                link(i, 1, nc.vector.tensor_reduce(rows[:, 0, :], s_shift[:, :, :], AX.X, ALU.max))
                nc.vector.tensor_tensor(s_shift[:, :, :], s_shift[:, :, :], bcast(rows[:, 0, :], N), ALU.subtract)\
                  .then_inc(s_shifted, 1)

            def att_norm(i):
                dve.wait_ge(exp_done, i + 1)
                link(i, 2, nc.vector.tensor_reduce(rows[:, 1, :], prob[:, :, :], AX.X, ALU.add))
                link(i, 3, nc.vector.reciprocal(rows[:, 2, :], rows[:, 1, :]))
                nc.vector.tensor_tensor(prob[:, :, :], prob[:, :, :], bcast(rows[:, 2, :], N), ALU.mult)\
                  .then_inc(prob_ready, 1)

            def att_copy(i):
                dve.wait_ge(prob_turned, i + 1)
                nc.vector.tensor_copy(prob_tr[:, :, :], att[1]).then_inc(prob_tr_ready, 1)

            def att_mix(i):
                dve.wait_ge(mixed, i + 1)
                nc.vector.tensor_copy(mix[:, :, :], att[0]).then_inc(mix_ready, 1)

            def att_y(i):
                dve.wait_ge(y_mm, i + 1)
                y = h_nat[:, bass.ds(i * QUAD, QUAD), :]
                link(i, 4, nc.vector.tensor_scalar(y, att[1], BG, None, ALU.add))
                nc.vector.bn_stats(bst[:, bass.ds(i, 1), :].rearrange("p a s -> p (a s)"),
                                   y.rearrange("p b n -> p (b n)")).then_inc(y_ready, 1)

            ATT = {26: att_scores, 29: att_norm, 31: att_copy, 33: att_mix, 35: att_y}
            AHEAD = 3

            def pass2_body(i, depth):
                for k in range(PER):
                    if k in PLAIN:
                        differences(1, i, k, depth)
                    for j, done in ended(i, k, LAG + AHEAD, depth):
                        evacuate(j, done, depth if k >= LAG + AHEAD else depth - 1)
                    for step, j in att_steps(ATT, i, k, depth):
                        step(j)

            pass2_body(0, 0)
            pass2_body(1, 1)
            with dve.Fori(2, NQ) as i:
                pass2_body(i, 2)
            for k in range(LAG + AHEAD):
                for j, done in ended(NQ, k, LAG + AHEAD, 2):
                    evacuate(j, done, 2)
            for step, j in att_rest(ATT):
                step(j)

            def then2(n, ins):
                ins.then_inc(bn2, 1)
                dve.wait_ge(bn2, n)

            dve.wait_ge(y_ready, NQ)
            then2(1, nc.vector.bn_aggr(bag[:, 0:2], bst[:, :, :].rearrange("p q s -> p (q s)")))
            nc.vector.tensor_scalar(bag[:, 2:3], bag[:, 1:2], EPS, None, ALU.add).then_inc(bn2_var, 1)
            dve.wait_ge(bn2_rstd, 1)
            then2(2, nc.vector.tensor_tensor(bag[:, 4:5], bag[:, 3:4], GG, ALU.mult))
            then2(3, nc.vector.tensor_tensor(bag[:, 5:6], bag[:, 0:1], bag[:, 4:5], ALU.mult))
            nc.vector.tensor_tensor(bag[:, 6:7], BEG, bag[:, 5:6], ALU.subtract).then_inc(bn2_ready, 1)
            final["vector"](dve, h_nat, bn2_ready)


def final_tiles(nc, sb, sem, diff, relu, psum):
    NS = 4
    NI = B // (4 * NS)
    store = [t[:, n // 2, BANK * (n % 2):BANK * (n % 2) + BANK] for t in diff for n in range(4)] + \
            [t[:, BANK * n:BANK * n + BANK] for t in relu for n in range(2)]
    store = [t.rearrange("p (b n) -> p b n", b=4) for t in store]
    X, H, Y, CEN, SQ, X1, HT = (store[NS * n:NS * n + NS] for n in range(7))
    H2T, MASK, DEN, HWN, MIN, OUT = (store[NS * n:NS * n + NS] for n in range(6))
    adjt = [t.bitcast(I32) for t in store[NS * 6:NS * 7]]
    small = sb("small", [128, NS, 6, 4])
    bank = [[psum[:, 2 * q + n, :].rearrange("p (b n) -> p b n", b=4) for n in range(2)] for q in range(NS)]

    x_in2, h_in2, x1_kept, h2_kept, h2_in, adjt_in, out_stored = (
        [sem(f"{n}{q}") for q in range(NS)]
        for n in ("x_in2_", "h_in2_", "x1_kept", "h2_kept", "h2_in", "adjt_in", "out_stored"))
    x_bt, y_act, y_leaky, o_mm, x1_ready, dve_a, cen_ready, sq_ready, var2_ready, rstd2_ready, h2_ready, \
        h2_turned, h2t_ready = (sem(n) for n in (
            "x_bt", "y_act", "y_leaky", "o_mm", "x1_ready", "dve_a", "cen_ready", "sq_ready", "var2_ready",
            "rstd2_ready", "h2_ready", "h2_turned", "h2t_ready"))
    mask_set, den_mm, den_low, hw_mm, dve_b, shifted, expd, hwn_ready, att_mm, neg_ready, neg_exp, elu_ready, \
        out_ready = (sem(n) for n in (
            "mask_set", "den_mm", "den_low", "hw_mm", "dve_b", "shifted", "expd", "hwn_ready", "att_mm",
            "neg_ready", "neg_exp", "elu_ready", "out_ready"))

    def at(i, q):
        return i * NS + q + 1

    def bc(v, n=128):
        return v.unsqueeze(2).broadcast_to([v.shape[0], v.shape[1], n])

    def graphs(i, q):
        return bass.ds((i * NS + q) * 4, 4)

    def flat(t):
        return t.rearrange("p b n -> p (b n)")

    def loop(eng, body):
        body(0, True)
        with eng.Fori(1, NI) as i:
            body(i, False)

    def sync(sp, x_n, out_n, adj_tn, h_nat, h_tr, y_ready):
        sp.wait_ge(y_ready, NQ)

        def loads_a(i, first):
            for q in range(NS):
                if not first:
                    sp.wait_ge(x1_ready, at(i - 1, q))
                    sp.wait_ge(o_mm, at(i - 1, q))
                sp.dma_start(X[q], x_n[:, graphs(i, q), :]).then_inc(x_in2[q], 16)
                sp.dma_start(H[q], h_tr[:, graphs(i, q), :]).then_inc(h_in2[q], 16)

        def stores_a(i):
            for q in range(NS):
                sp.wait_ge(x1_ready, at(i, q))
                sp.dma_start(h_nat[:, graphs(i, q), :], X1[q]).then_inc(x1_kept[q], 16)

        loads_a(0, True)
        with sp.Fori(1, NI) as i:
            loads_a(i, False)
            stores_a(i - 1)
        stores_a(NI - 1)
        for q in range(NS):
            sp.wait_ge(x1_kept[q], NI * 16)
            sp.wait_ge(h2_kept[q], NI * 16)

        def loads_b(i, first):
            for q in range(NS):
                if not first:
                    sp.wait_ge(att_mm, at(i - 1, q))
                    sp.wait_ge(mask_set, at(i - 1, q))
                sp.dma_start(H2T[q], h_tr[:, graphs(i, q), :]).then_inc(h2_in[q], 16)
                sp.dma_start(adjt[q], adj_tn[:, graphs(i, q), :]).then_inc(adjt_in[q], 16)

        def stores(i):
            for q in range(NS):
                sp.wait_ge(out_ready, at(i, q))
                sp.dma_start(out_n[:, graphs(i, q), :], OUT[q]).then_inc(out_stored[q], 16)

        loads_b(0, True)
        with sp.Fori(1, NI) as i:
            loads_b(i, False)
            stores(i - 1)
        stores(NI - 1)
        for q in range(NS):
            sp.wait_ge(out_stored[q], 16 * NI)

    def gpsimd(pool, bt_sb, minus_half):
        def body_a(i, first):
            for q in range(NS):
                pool.wait_ge(x_in2[q], (i + 1) * 16)
                nc.gpsimd.tensor_tensor(X[q], X[q], bt_sb[:, :].unsqueeze(1).broadcast_to([128, 4, 128]),
                                        ALU.add).then_inc(x_bt, 1)
            for q in range(NS):
                pool.wait_ge(var2_ready, at(i, q))
                nc.gpsimd.tensor_tensor(small[:, q, 3, :], small[:, q, 2, :], minus_half[:, 0:4], ALU.pow)\
                  .then_inc(rstd2_ready, 1)

        loop(pool, body_a)

    def scalar(act, bag, h_nat, h_tr):
        def body_a(i, first):
            for q in range(NS):
                if not first:
                    act.wait_ge(o_mm, at(i - 1, q))
                nc.scalar.activation(Y[q], h_nat[:, graphs(i, q), :], ACT.Identity,
                                     bias=bag[:, 6:7], scale=bag[:, 4:5]).then_inc(y_act, 1)
            for q in range(NS):
                act.wait_ge(cen_ready, at(i, q))
                nc.scalar.activation(SQ[q], CEN[q], ACT.Square).then_inc(sq_ready, 1)
            for q in range(NS):
                act.wait_ge(h2_turned, at(i, q))
                if not first:
                    act.wait_ge(h2_kept[q], i * 16)
                nc.scalar.copy(HT[q], bank[q][1]).then_inc(h2t_ready, 1)
            for q in range(NS):
                act.wait_ge(h2t_ready, at(i, q))
                act.dma_start(h_tr[:, graphs(i, q), :], HT[q]).then_inc(h2_kept[q], 16)

        def body_b(i, first):
            for q in range(NS):
                act.wait_ge(den_mm, at(i, q))
                if not first:
                    act.wait_ge(att_mm, at(i - 1, q))
                nc.scalar.mul(DEN[q], bank[q][0], SLOPE1).then_inc(den_low, 1)
            for q in range(NS):
                act.wait_ge(shifted, at(i, q))
                nc.scalar.activation(DEN[q], DEN[q], ACT.Exp).then_inc(expd, 1)
            for q in range(NS):
                act.wait_ge(att_mm, at(i, q))
                if not first:
                    act.wait_ge(out_ready, at(i - 1, q))
                nc.scalar.activation(MIN[q], bank[q][1], ACT.Relu, scale=-1.0).then_inc(neg_ready, 1)
            for q in range(NS):
                act.wait_ge(neg_ready, at(i, q))
                nc.scalar.activation(MIN[q], MIN[q], ACT.Exp, scale=-1.0).then_inc(neg_exp, 1)

        loop(act, body_a)
        for q in range(NS):
            act.wait_ge(x1_kept[q], NI * 16)
            act.wait_ge(h2_kept[q], NI * 16)
        loop(act, body_b)

    def tensor(pe, wt1, wt2, l1w, w1a, w2a, ident):
        def body_a(i, first):
            for q in range(NS):
                pe.wait_ge(h_in2[q], (i + 1) * 16)
                pe.wait_ge(y_leaky, at(i, q))
                if not first:
                    pe.wait_ge(x1_ready, at(i - 1, q))
                for b in range(4):
                    nc.tensor.matmul(bank[q][0][:, b, :], H[q][:, b, :], wt1[:, :], start=True, stop=False)
                    last = nc.tensor.matmul(bank[q][0][:, b, :], Y[q][:, b, :], wt2[:, :], start=False, stop=True)
                last.then_inc(o_mm, 1)
            for q in range(NS):
                pe.wait_ge(h2_ready, at(i, q))
                if not first:
                    pe.wait_ge(h2t_ready, at(i - 1, q))
                for b in range(4):
                    last = nc.tensor.transpose(bank[q][1][:, b, :], CEN[q][:, b, :], ident[:, :])
                last.then_inc(h2_turned, 1)

        def body_b(i, first):
            for q in range(NS):
                pe.wait_ge(h2_in[q], (i + 1) * 16)
                if first:
                    pe.wait_ge(h2t_ready, NI * NS)
                else:
                    pe.wait_ge(out_ready, at(i - 1, q))
                for b in range(4):
                    nc.tensor.matmul(bank[q][0][:, b, :], w1a[:, :], H2T[q][:, b, :], start=True, stop=False)
                    last = nc.tensor.matmul(bank[q][0][:, b, :], H2T[q][:, b, :], w2a[:, :], start=False, stop=True)
                last.then_inc(den_mm, 1)
            for q in range(NS):
                for b in range(4):
                    last = nc.tensor.matmul(bank[q][1][:, b, :], H2T[q][:, b, :], l1w[:, :], start=True, stop=True)
                last.then_inc(hw_mm, 1)
            for q in range(NS):
                pe.wait_ge(hwn_ready, at(i, q))
                for b in range(4):
                    last = nc.tensor.matmul(bank[q][1][:, b, :], DEN[q][:, b, :], HWN[q][:, b, :], start=True, stop=True)
                last.then_inc(att_mm, 1)

        loop(pe, body_a)
        loop(pe, body_b)

    def vector(dve, h_nat, bn2_ready):
        LINKS_A, LINKS_B = 3, 5

        def body_a(i, first):
            steps = iter(range(1, LINKS_A * NS + 1))

            def link(ins):
                ins.then_inc(dve_a, 1)
                dve.wait_ge(dve_a, i * LINKS_A * NS + next(steps))

            for q in range(NS):
                dve.wait_ge(y_act, at(i, q))
                nc.vector.scalar_tensor_tensor(Y[q], Y[q], SLOPE0, Y[q], ALU.mult, ALU.max).then_inc(y_leaky, 1)
            for q in range(NS):
                sm = small[:, q]
                x1 = X1[q]
                if not first:
                    dve.wait_ge(x1_kept[q], i * 16)
                dve.wait_ge(o_mm, at(i, q))
                dve.wait_ge(x_bt, at(i, q))
                nc.vector.tensor_tensor(x1, bank[q][0], X[q], ALU.add).then_inc(x1_ready, 1)
                dve.wait_ge(x1_ready, at(i, q))
                link(nc.vector.tensor_reduce(sm[:, 0, :], x1, AX.X, ALU.add))
                link(nc.vector.tensor_scalar(sm[:, 0, :], sm[:, 0, :], 1.0 / C, None, ALU.mult))
                nc.vector.tensor_tensor(CEN[q], x1, bc(sm[:, 0, :]), ALU.subtract).then_inc(cen_ready, 1)
            for q in range(NS):
                sm = small[:, q]
                dve.wait_ge(sq_ready, at(i, q))
                link(nc.vector.tensor_reduce(sm[:, 1, :], SQ[q], AX.X, ALU.add))
                nc.vector.tensor_scalar(sm[:, 2, :], sm[:, 1, :], 1.0 / C, EPS, ALU.mult, ALU.add).then_inc(var2_ready, 1)
            for q in range(NS):
                dve.wait_ge(rstd2_ready, at(i, q))
                nc.vector.scalar_tensor_tensor(CEN[q], CEN[q], 0.0, bc(small[:, q, 3, :]), ALU.max, ALU.mult)\
                  .then_inc(h2_ready, 1)

        def body_b(i, first):
            steps = iter(range(1, LINKS_B * NS + 1))

            def link(ins):
                ins.then_inc(dve_b, 1)
                dve.wait_ge(dve_b, i * LINKS_B * NS + next(steps))

            for q in range(NS):
                dve.wait_ge(adjt_in[q], (i + 1) * 16)
                nc.vector.tensor_scalar(MASK[q], adjt[q], 0.0, NEG, ALU.is_le, ALU.mult).then_inc(mask_set, 1)
            for q in range(NS):
                sm = small[:, q]
                dve.wait_ge(den_low, at(i, q))
                link(nc.vector.tensor_tensor(DEN[q], bank[q][0], DEN[q], ALU.max))
                dve.wait_ge(mask_set, at(i, q))
                link(nc.vector.tensor_tensor(DEN[q], DEN[q], MASK[q], ALU.add))
                link(nc.vector.tensor_reduce(sm[:, 0, :], DEN[q], AX.X, ALU.max))
                nc.vector.tensor_tensor(DEN[q], DEN[q], bc(sm[:, 0, :]), ALU.subtract).then_inc(shifted, 1)
            for q in range(NS):
                sm = small[:, q]
                dve.wait_ge(expd, at(i, q))
                link(nc.vector.tensor_reduce(sm[:, 1, :], DEN[q], AX.X, ALU.add))
                link(nc.vector.reciprocal(sm[:, 2, :], sm[:, 1, :]))
                dve.wait_ge(hw_mm, at(i, q))
                nc.vector.tensor_tensor(HWN[q], bank[q][1], bc(sm[:, 2, :]), ALU.mult).then_inc(hwn_ready, 1)
            for q in range(NS):
                dve.wait_ge(neg_exp, at(i, q))
                if not first:
                    dve.wait_ge(out_stored[q], i * 16)
                nc.vector.scalar_tensor_tensor(OUT[q], bank[q][1], 0.0, MIN[q], ALU.max, ALU.add).then_inc(elu_ready, 1)
            for q in range(NS):
                dve.wait_ge(elu_ready, at(i, q))
                nc.vector.scalar_tensor_tensor(OUT[q], OUT[q], -1.0, h_nat[:, graphs(i, q), :], ALU.add, ALU.add)\
                  .then_inc(out_ready, 1)

        dve.wait_ge(bn2_ready, 1)
        loop(dve, body_a)
        dve.wait_ge(h2t_ready, NI * NS)
        for q in range(NS):
            dve.wait_ge(x1_kept[q], NI * 16)
            dve.wait_ge(h2_kept[q], NI * 16)
        loop(dve, body_b)

    return dict(sync=sync, gpsimd=gpsimd, scalar=scalar, tensor=tensor, vector=vector)


def pair_table():
    table = np.zeros((N, len(BY_MAX) * WIDE), np.float32)
    for m, k in enumerate(BY_MAX):
        at = m * WIDE
        for blk in CHUNKS[k]:
            j0, n = strip(blk)
            for i in range(j0 - BLK, j0):
                table[i, at:at + n] -= 1
                table[np.arange(j0, N), np.arange(at, at + n)] -= 1
                at += n
    return table


def kernel(**inputs):
    import concourse.bacc as _bacc
    from concourse.bass_utils import run_bass_kernel_spmd as _run

    a = {k: np.ascontiguousarray(v) for k, v in inputs.items()}
    wt = a["L0_gnn_Wt"]
    two = lambda v: np.concatenate([v, v])
    l1a = a["L1_gnn_a"][:, 0]
    cols = np.stack([two(a["L0_gnn_g1"]), two(a["L0_gnn_be1"]), two(a["L0_gnn_b1"]), two(a["L0_gnn_W2"][0]),
                     a["L0_gnn_bg"], a["L0_gnn_gg"], a["L0_gnn_beg"], l1a[:C], l1a[C:],
                     np.broadcast_to(a["L0_gnn_b2"], (128,))], axis=1)
    node = np.arange(128)
    half = np.where(node[:, None, None] // BLK == np.arange(NBLK)[None, :, None], 0.5, 0.0)
    arrays = {
        "x": a["x"], "adj": a["adj"], "adj_t": a["adj"].transpose(0, 2, 1),
        "w1": a["L0_gnn_W1"], "w1_tt": np.concatenate([a["L0_gnn_W1"].T] * 2, axis=1),
        "wg_t": a["L0_gnn_Wg"].T, "wt1_t": wt[:, :C].T, "wt2_t": wt[:, C:].T,
        "l1_w": a["L1_gnn_W"], "l1_wt": a["L1_gnn_W"].T, "cols": cols,
        "bt_rows": np.broadcast_to(a["L0_gnn_bt"], (128, C)),
        "ident_in": np.eye(128, dtype=np.float32),
        "fold_in": (node[:, None] % MID == node[None, :] % MID).astype(np.float32),
        "pair_nodes_in": pair_table(),
        "half_in": np.broadcast_to(half, (128, NBLK, BLK)).astype(np.float32),
    }
    arrays = {k: np.ascontiguousarray(v) for k, v in arrays.items()}
    nc = _bacc.Bacc("TRN2", target_bir_lowering=False, num_devices=1)
    aps = [nc.dram_tensor(k, v.shape, mybir.dt.from_np(v.dtype), kind="ExternalInput").ap() for k, v in arrays.items()]
    out = nc.dram_tensor("out", (B, N, C), F32, kind="ExternalOutput").ap()
    two_layers(nc, *aps, out)
    r = _run(nc, [arrays], core_ids=[0])
    return r.results[0]["out"]
```
